# Optimizing a Trainium2 kernel written in Bass

```python
import numpy as np
import jax
import jax.numpy as jnp

def _softmax(x, axis=-1):
    return jax.nn.softmax(x, axis=axis)

def _gelu(x):
    return jax.nn.gelu(x, approximate=True)

def _silu(x):
    return jax.nn.silu(x)

def _sigmoid(x):
    return jax.nn.sigmoid(x)

def _layernorm(x, axis=-1, eps=1e-05):
    m = jnp.mean(x, axis=axis, keepdims=True)
    v = jnp.var(x, axis=axis, keepdims=True)
    return (x - m) / jnp.sqrt(v + eps)

def _scatter_add(tgt, idx, src, axis=0):
    return tgt.at[idx].add(src)

def _segment_sum(src, seg, n):
    return jax.ops.segment_sum(src, seg, n)
kernel_name = 'mk_xattn_ffn_d1_seqx_r8_4f8848'

def setup_inputs(seed: int=0):
    np.random.seed(seed)
    _w = jnp.asarray

    def _rec_inputs():
        import jax
        import jax.numpy as jnp
        _rk = jax.random.key(seed)
        x = 4.136e-05 + 0.9999 * jax.random.normal(jax.random.fold_in(_rk, 1), (4, 256, 256), jnp.float32)
        _lenS = 256 - jax.random.randint(jax.random.fold_in(_rk, 7), (4,), 0, max(1, 256 // 4) + 1, jnp.int32)
        _lenS2 = 256 - jax.random.randint(jax.random.fold_in(_rk, 8), (4,), 0, max(1, 256 // 4) + 1, jnp.int32)
        _ctx_1024P = jax.random.normal(jax.random.fold_in(_rk, 11), (4, 16, 128), jnp.float32)
        _ctx_1024c = jax.random.dirichlet(jax.random.fold_in(_rk, 511), 0.3 * jnp.ones((16,), jnp.float32), (4, 256))
        _ctx_1024t = jnp.einsum('bsk,bkd->bsd', _ctx_1024c, _ctx_1024P)
        _ctx_1024t = _ctx_1024t * jax.lax.rsqrt(jnp.mean(jnp.square(_ctx_1024t)) + 1e-12) * 0.953939
        ctx_1024 = -0.000292821 + 1.00034 * (_ctx_1024t + 0.3 * jax.random.normal(jax.random.fold_in(_rk, 611), (4, 256, 128), jnp.float32))
        return (x, ctx_1024)
    x, ctx_1024 = _rec_inputs()

    def _L0_xattn_setup():
        import jax, jax.numpy as jnp
        import numpy as np
        import math
        B, L, DM = (2, 256, 128)
        DS, DC, EXP = (16, 4, 2)
        DI = EXP * DM
        DR = math.ceil(DM / 16)
        DT_MIN, DT_MAX, DT_FLOOR = (0.001, 0.1, 0.0001)

        def _ssm_forward(hidden_states, z, in_proj_w, conv_w, conv_b, x_proj_w, dt_proj_w, dt_proj_b, A_log, D):
            b = hidden_states.shape[0]
            x = jnp.einsum('ed,bld->bel', in_proj_w, hidden_states)
            xp = jnp.pad(x, ((0, 0), (0, 0), (DC - 1, 0)))
            xc = jax.lax.conv_general_dilated(xp, conv_w[:, None, :], window_strides=(1,), padding='VALID', dimension_numbers=('NCH', 'OIH', 'NCH'), feature_group_count=DI)
            u = jax.nn.silu(xc + conv_b[None, :, None])
            x_dbl = jnp.einsum('ke,bel->bkl', x_proj_w, u)
            dt_lo = x_dbl[:, :DR]
            Bm = x_dbl[:, DR:DR + DS]
            Cm = x_dbl[:, DR + DS:]
            delta = jax.nn.softplus(jnp.einsum('er,brl->bel', dt_proj_w, dt_lo) + dt_proj_b[None, :, None])
            A = -jnp.exp(A_log)

            def step(state, xs):
                d_t, B_t, C_t, u_t = xs
                dA = jnp.exp(d_t[..., None] * A)
                state = state * dA + (d_t * u_t)[..., None] * B_t[:, None, :]
                y_t = jnp.einsum('ben,bn->be', state, C_t)
                return (state, y_t)
            xs = (jnp.moveaxis(delta, -1, 0), jnp.moveaxis(Bm, -1, 0), jnp.moveaxis(Cm, -1, 0), jnp.moveaxis(u, -1, 0))
            state0 = jnp.zeros((b, DI, DS), delta.dtype)
            _, ys = jax.lax.scan(step, state0, xs)
            y = jnp.moveaxis(ys, 0, -1)
            y = y + D[None, :, None] * u
            y = y * jax.nn.silu(z)
            return jnp.swapaxes(y, 1, 2)
        key = jax.random.key(seed)
        ks = jax.random.split(key, 8)
        hidden_states = jax.random.normal(ks[0], (B, L, DM), jnp.float32)
        z = jax.random.normal(ks[1], (B, DI, L), jnp.float32)
        in_proj_w = jax.random.normal(ks[2], (DI, DM), jnp.float32) * DM ** (-0.5)
        conv_w = jax.random.normal(ks[3], (DI, DC), jnp.float32) * DC ** (-0.5)
        conv_b = jnp.zeros((DI,), jnp.float32)
        x_proj_w = jax.random.normal(ks[4], (DR + 2 * DS, DI), jnp.float32) * DI ** (-0.5)
        dt_std = DR ** (-0.5)
        dt_proj_w = jax.random.uniform(ks[5], (DI, DR), jnp.float32, -dt_std, dt_std)
        dt = jnp.exp(jax.random.uniform(ks[6], (DI,), jnp.float32) * (math.log(DT_MAX) - math.log(DT_MIN)) + math.log(DT_MIN))
        dt = jnp.clip(dt, DT_FLOOR)
        dt_proj_b = dt + jnp.log(-jnp.expm1(-dt))
        A_log = jnp.log(jnp.broadcast_to(jnp.arange(1, DS + 1, dtype=jnp.float32), (DI, DS)))
        D = jnp.ones((DI,), jnp.float32)
        return dict(hidden_states=hidden_states, z=z, in_proj_w=in_proj_w, conv_w=conv_w, conv_b=conv_b, x_proj_w=x_proj_w, dt_proj_w=dt_proj_w, dt_proj_b=dt_proj_b, A_log=A_log, D=D)
    _L0_xattn_all = _L0_xattn_setup()
    _L0_xattn_in = {k: v for k, v in _L0_xattn_all.items() if k in ('in_proj_w', 'conv_w', 'conv_b', 'x_proj_w', 'dt_proj_w', 'dt_proj_b', 'A_log', 'D')}
    del _L0_xattn_all

    def _L0_ffn_setup():
        import jax, jax.numpy as jnp
        import numpy as np
        D_MODEL = 256
        D_HIDDEN = 176
        NUM_SHARED = 2
        NUM_ROUTED = 32
        TOP_K = 6

        def _expert_apply(xf, w1, b1, w2, b2):
            return jnp.maximum(xf @ w1 + b1, 0.0) @ w2 + b2
        key = jax.random.key(seed)
        ks = jax.random.split(key, 11)
        d, h = (D_MODEL, D_HIDDEN)
        s1 = 1.0 / np.sqrt(d)
        s2 = 1.0 / np.sqrt(h)
        x = jax.random.normal(ks[0], (2, 256, d), dtype=jnp.float32)
        sw1 = jax.random.uniform(ks[1], (NUM_SHARED, d, h), jnp.float32, -s1, s1)
        sb1 = jax.random.uniform(ks[2], (NUM_SHARED, h), jnp.float32, -s1, s1)
        sw2 = jax.random.uniform(ks[3], (NUM_SHARED, h, d), jnp.float32, -s2, s2)
        sb2 = jax.random.uniform(ks[4], (NUM_SHARED, d), jnp.float32, -s2, s2)
        rw1 = jax.random.uniform(ks[5], (NUM_ROUTED, d, h), jnp.float32, -s1, s1)
        rb1 = jax.random.uniform(ks[6], (NUM_ROUTED, h), jnp.float32, -s1, s1)
        rw2 = jax.random.uniform(ks[7], (NUM_ROUTED, h, d), jnp.float32, -s2, s2)
        rb2 = jax.random.uniform(ks[8], (NUM_ROUTED, d), jnp.float32, -s2, s2)
        router_w = jax.random.uniform(ks[9], (d, NUM_ROUTED), jnp.float32, -s1, s1)
        router_b = jax.random.uniform(ks[10], (NUM_ROUTED,), jnp.float32, -s1, s1)
        return {'x': x, 'sw1': sw1, 'sb1': sb1, 'sw2': sw2, 'sb2': sb2, 'rw1': rw1, 'rb1': rb1, 'rw2': rw2, 'rb2': rb2, 'router_w': router_w, 'router_b': router_b}
    _L0_ffn_all = _L0_ffn_setup()
    _L0_ffn_in = {k: v for k, v in _L0_ffn_all.items() if k in ('sw1', 'sb1', 'sw2', 'sb2', 'rw1', 'rb1', 'rw2', 'rb2', 'router_w', 'router_b')}
    del _L0_ffn_all
    return {'x': x, 'ctx_1024': ctx_1024, 'L0_xattn_in_proj_w': _L0_xattn_in['in_proj_w'], 'L0_xattn_conv_w': _L0_xattn_in['conv_w'], 'L0_xattn_conv_b': _L0_xattn_in['conv_b'], 'L0_xattn_x_proj_w': _L0_xattn_in['x_proj_w'], 'L0_xattn_dt_proj_w': _L0_xattn_in['dt_proj_w'], 'L0_xattn_dt_proj_b': _L0_xattn_in['dt_proj_b'], 'L0_xattn_A_log': _L0_xattn_in['A_log'], 'L0_xattn_D': _L0_xattn_in['D'], 'L0_ffn_sw1': _L0_ffn_in['sw1'], 'L0_ffn_sb1': _L0_ffn_in['sb1'], 'L0_ffn_sw2': _L0_ffn_in['sw2'], 'L0_ffn_sb2': _L0_ffn_in['sb2'], 'L0_ffn_rw1': _L0_ffn_in['rw1'], 'L0_ffn_rb1': _L0_ffn_in['rb1'], 'L0_ffn_rw2': _L0_ffn_in['rw2'], 'L0_ffn_rb2': _L0_ffn_in['rb2'], 'L0_ffn_router_w': _L0_ffn_in['router_w'], 'L0_ffn_router_b': _L0_ffn_in['router_b']}

def reference(x, ctx_1024, L0_xattn_in_proj_w, L0_xattn_conv_w, L0_xattn_conv_b, L0_xattn_x_proj_w, L0_xattn_dt_proj_w, L0_xattn_dt_proj_b, L0_xattn_A_log, L0_xattn_D, L0_ffn_sw1, L0_ffn_sb1, L0_ffn_sw2, L0_ffn_sb2, L0_ffn_rw1, L0_ffn_rb1, L0_ffn_rw2, L0_ffn_rb2, L0_ffn_router_w, L0_ffn_router_b):
    import jax
    import jax.numpy as jnp

    def _L0_xattn_ref(hidden_states, z, in_proj_w, conv_w, conv_b, x_proj_w, dt_proj_w, dt_proj_b, A_log, D):
        import jax, jax.numpy as jnp
        import numpy as np
        import math
        B, L, DM = (2, 256, 128)
        DS, DC, EXP = (16, 4, 2)
        DI = EXP * DM
        DR = math.ceil(DM / 16)
        DT_MIN, DT_MAX, DT_FLOOR = (0.001, 0.1, 0.0001)

        def _ssm_forward(hidden_states, z, in_proj_w, conv_w, conv_b, x_proj_w, dt_proj_w, dt_proj_b, A_log, D):
            b = hidden_states.shape[0]
            x = jnp.einsum('ed,bld->bel', in_proj_w, hidden_states)
            xp = jnp.pad(x, ((0, 0), (0, 0), (DC - 1, 0)))
            xc = jax.lax.conv_general_dilated(xp, conv_w[:, None, :], window_strides=(1,), padding='VALID', dimension_numbers=('NCH', 'OIH', 'NCH'), feature_group_count=DI)
            u = jax.nn.silu(xc + conv_b[None, :, None])
            x_dbl = jnp.einsum('ke,bel->bkl', x_proj_w, u)
            dt_lo = x_dbl[:, :DR]
            Bm = x_dbl[:, DR:DR + DS]
            Cm = x_dbl[:, DR + DS:]
            delta = jax.nn.softplus(jnp.einsum('er,brl->bel', dt_proj_w, dt_lo) + dt_proj_b[None, :, None])
            A = -jnp.exp(A_log)

            def step(state, xs):
                d_t, B_t, C_t, u_t = xs
                dA = jnp.exp(d_t[..., None] * A)
                state = state * dA + (d_t * u_t)[..., None] * B_t[:, None, :]
                y_t = jnp.einsum('ben,bn->be', state, C_t)
                return (state, y_t)
            xs = (jnp.moveaxis(delta, -1, 0), jnp.moveaxis(Bm, -1, 0), jnp.moveaxis(Cm, -1, 0), jnp.moveaxis(u, -1, 0))
            state0 = jnp.zeros((b, DI, DS), delta.dtype)
            _, ys = jax.lax.scan(step, state0, xs)
            y = jnp.moveaxis(ys, 0, -1)
            y = y + D[None, :, None] * u
            y = y * jax.nn.silu(z)
            return jnp.swapaxes(y, 1, 2)
        return _ssm_forward(hidden_states, z, in_proj_w, conv_w, conv_b, x_proj_w, dt_proj_w, dt_proj_b, A_log, D)

    def _L0_ffn_ref(x, sw1, sb1, sw2, sb2, rw1, rb1, rw2, rb2, router_w, router_b):
        import jax, jax.numpy as jnp
        import numpy as np
        D_MODEL = 256
        D_HIDDEN = 176
        NUM_SHARED = 2
        NUM_ROUTED = 32
        TOP_K = 6

        def _expert_apply(xf, w1, b1, w2, b2):
            return jnp.maximum(xf @ w1 + b1, 0.0) @ w2 + b2
        B, S, d = x.shape
        flat = x.reshape(-1, d)
        T = flat.shape[0]

        def sh_body(acc, p):
            w1, b1, w2, b2 = p
            return (acc + _expert_apply(flat, w1, b1, w2, b2), None)
        shared_out, _ = jax.lax.scan(sh_body, jnp.zeros_like(flat), (sw1, sb1, sw2, sb2))
        shared_out = shared_out / NUM_SHARED
        logits = flat @ router_w + router_b
        probs = jax.nn.softmax(logits, axis=-1)
        topk_p, topk_i = jax.lax.top_k(probs, TOP_K)
        topk_p = topk_p / jnp.sum(topk_p, axis=-1, keepdims=True)
        gates = jnp.zeros((T, NUM_ROUTED), dtype=flat.dtype)
        gates = gates.at[jnp.arange(T)[:, None], topk_i].add(topk_p)

        def r_body(acc, p):
            w1, b1, w2, b2, g = p
            return (acc + g[:, None] * _expert_apply(flat, w1, b1, w2, b2), None)
        routed_out, _ = jax.lax.scan(r_body, jnp.zeros_like(flat), (rw1, rb1, rw2, rb2, gates.T))
        return (shared_out + routed_out).reshape(B, S, d)
    x = x + _L0_xattn_ref(ctx_1024, _layernorm(x, axis=-1), L0_xattn_in_proj_w, L0_xattn_conv_w, L0_xattn_conv_b, L0_xattn_x_proj_w, L0_xattn_dt_proj_w, L0_xattn_dt_proj_b, L0_xattn_A_log, L0_xattn_D)
    x = x + _L0_ffn_ref(_layernorm(x, axis=-1), L0_ffn_sw1, L0_ffn_sb1, L0_ffn_sw2, L0_ffn_sb2, L0_ffn_rw1, L0_ffn_rb1, L0_ffn_rw2, L0_ffn_rb2, L0_ffn_router_w, L0_ffn_router_b)
    return x

_drawn_inputs = setup_inputs


def setup_inputs(seed=0):
    import zlib

    import numpy as np

    out = dict(_drawn_inputs(seed))
    spreads = {'L0_xattn_conv_b': (0.0, 0.1), 'L0_xattn_D': (1.0, 0.2)}
    factors = {'L0_xattn_dt_proj_w': 5.179,
     'L0_ffn_sb1': 5.526,
     'L0_ffn_rb1': 8.0,
     'L0_ffn_rb2': 3.357,
     'L0_ffn_router_b': 3.079}
    for name, (base, spread) in spreads.items():
        noise = np.random.default_rng([zlib.crc32(name.encode()), seed]).standard_normal(out[name].shape)
        drawn = base * np.exp(spread * noise) if base else spread * noise
        out[name] = jnp.asarray(drawn.astype(out[name].dtype))
    for name, factor in factors.items():
        out[name] = (out[name] * factor).astype(out[name].dtype)
    return out
```

```python
from contextlib import ExitStack

import concourse.bass as bass
from concourse import mybir

F32 = mybir.dt.float32
BF16 = mybir.dt.bfloat16
ALU = mybir.AluOpType
ACT = mybir.ActivationFunctionType
AX = mybir.AxisListType

P = 128
B, L, DX = 4, 256, 256
DC_IN = 128
KD = DX // P
NS, DR, KC = 16, 8, 4
NR, NSH, HID, TOPK = 32, 2, 176, 6
NT_R = NR * HID // P
NT = -(-(NR + NSH) * HID // P)
NP = (NT + 1) // 2
NC = NS // 2
EPS = 1e-5
LOWEST = -3.0e38
HUGE = 3.0e38
WCH = 4

PAR = {}
_at = 0
for _name, _n in (("win", DX), ("xbc", KD * 3 * 2 * NS), ("xdt", KD * DR), ("cw", KD * KC), ("cb", KD), ("dtb", KD),
                  ("alog", KD * NS), ("dd", KD), ("rw", KD * NR), ("rb", NR), ("b1", NT), ("ident", P)):
    PAR[_name] = (_at, _at + _n)
    _at += _n
NPAR = _at

STEPS = [("xin", 0), ("conv", 0), ("u", 1), ("xdbl", 2), ("split", 2), ("dt", 3), ("delta", 3), ("zgate", 4)]
STEPS += [(("chunk", c), 4 + (c * 14) // 8) for c in range(NC)]
STEPS += [("x1", 18), ("mean", 19), ("centre", 19), ("var", 20), ("norm", 20), ("logits", 21), ("gates", 21),
          ("turn", 23)]


def xattn_ffn_kernel(nc: bass.Bass, xT_d, xr_d, ctx_d, par_d, small_d, wall_d, selg_d, selbc_d, out_d):
    ctx = ExitStack()
    with ctx:
        def sb(name, shape, dt=F32):
            return ctx.enter_context(nc.sbuf_tensor(name, shape, dt))

        def ps(name, shape, dt=F32):
            return ctx.enter_context(nc.psum_tensor(name, shape, dt))

        def sem(name):
            return ctx.enter_context(nc.semaphore(name))

        xT = sb("xT", [P, KD, B, L])
        xr = sb("xr", [P, KD, B, DX])
        ctxT = sb("ctxT", [P, B, L])
        par = sb("par", [P, NPAR])
        small = sb("small", [NR + NSH, 2 * DX])
        wall = sb("wall", [P, NT, 4 * P])
        selg = sb("selg", [3 * NR, NT_R, P], BF16)
        selbc = sb("selbc", [3 * 2 * NS, 2 * NS, P], BF16)

        def pv(name):
            return par[:, PAR[name][0]:PAR[name][1]]

        win, cb, dtb, dd, rb, b1, ident = (pv(n) for n in ("win", "cb", "dtb", "dd", "rb", "b1", "ident"))
        xbc = pv("xbc").rearrange("p (k m) -> p k m", k=KD)
        xdt = pv("xdt").rearrange("p (k m) -> p k m", k=KD)
        cw = pv("cw").rearrange("p (k m) -> p k m", k=KD)
        rw = pv("rw").rearrange("p (k m) -> p k m", k=KD)
        dtw = small[0:DR, 0:DX]
        b2x = small[:, DX:2 * DX]

        identb = sb("identb", [P, P], BF16)
        meanw = sb("meanw", [P, P])
        aneg = sb("aneg", [P, KD * NS])
        epsc = sb("epsc", [P, 1])
        st6 = sb("st6", [P, KD * B, 6])
        mv = sb("mv", [P, KD, B, 2])
        rs1 = sb("rs1", [P, KD, B, 1])
        t1 = sb("t1", [P, KD, B, 1])
        cv = sb("cv", [P, KD, L])
        e1 = sb("e1", [P, KD, L])
        rec = sb("rec", [P, KD, L])
        u = sb("u", [P, KD, L])
        bcx = sb("bcx", [96, L])
        bcr = sb("bcr", [96, L])
        bcm = sb("bcm", [96, L], BF16)
        bcs = sb("bcs", [96, L], BF16)
        dtl = sb("dtl", [DR, L])
        v, sp = rec, e1
        delta = sb("delta", [P, KD, L])
        du = sb("du", [P, KD, L])
        zz = cv
        sz = sb("sz", [P, KD, L])
        dA = sb("dA", [P, KD, 2 * L])
        bu = sb("bu", [P, KD, 2 * L])
        pr = sb("pr", [P, KD, 2 * L])
        ya = sb("ya", [P, KD, 2 * L])
        y = sb("y", [P, KD, L])
        x1 = sb("x1", [P, 2, KD, L])
        xc = sb("xc", [P, KD, L])
        sq = y
        r2 = sb("r2", [P, L])
        n1 = sb("n1", [P, L])
        n2 = sb("n2", [P, L])
        xs = sb("xs", [P, KD, L])
        xn = sb("xn", [P, 2, KD, L])
        lg = sb("lg", [P, 2, NR + 2])
        m8 = sb("m8", [P, 2, 8])
        nm = sb("nm", [P, 2])
        sink = sb("sink", [P, 1])
        rep = sb("rep", [P, 2, NR + 2])
        ex = sb("ex", [P, 2, NR])
        mask = sb("mask", [P, 2, NR])
        em = sb("em", [P, 2, NR])
        sm = sb("sm", [P, 2])
        rsm = sb("rsm", [P, 2])
        g34 = sb("g34", [P, 2, NR + NSH])
        gr = sb("gr", [P, 2, NR])
        g3 = sb("g3", [P, 2, 3, NR], BF16)
        gst = sb("gst", [3 * NR, 2, L], BF16)
        gT = sb("gT", [NR + NSH, L])
        r = sb("r", [P, 2, 2, L])
        hg = sb("hg", [P, 2, 2, L])
        ot = sb("ot", [P, KD, L])

        z = [ps(f"z{i}", [P, 2, L]) for i in range(2)]
        gb = [ps(f"gb{i}", [P, 2, L]) for i in range(2)]
        acc = ps("acc", [P, KD, L])
        bb = ps("bb", [P, 2, L])
        cc = ps("cc", [P, 2, L])
        misc = ps("misc", [P, 2, L])
        miscb = misc[:].rearrange("p a b -> p (a b)").bitcast(BF16)

        ld_ctx, ld_par, ld_xr, ld_xT, ld_sel, ld_selg = (sem(n) for n in
                                                         ("ld_ctx", "ld_par", "ld_xr", "ld_xT", "ld_sel", "ld_selg"))
        ld_w = [sem(f"ld_w{i}") for i in range(-(-NT // WCH))]
        dve_step, act_step, pool_step = sem("dve_step"), sem("act_step"), sem("pool_step")
        aexp_done, aneg_done, const_done = sem("aexp_done"), sem("aneg_done"), sem("const_done")
        var1_done, ln1_done, rstd1_done = sem("var1_done"), sem("ln1_done"), sem("rstd1_done")
        names = ["xin_done", "conv_done", "econv_done", "u_done", "xdbl_done", "dtl_done", "bcs_done", "dt_done",
                 "v_done", "sp_done", "delta_done", "zz_done", "ez_done", "b_ready", "c_ready", "bu_done", "da_ready",
                 "scan_done", "prod_done", "y_folded", "x1_done", "xs_done", "mean_done", "xc_done", "sq_done", "var_done", "r2_done",
                 "xn_done", "logits_done", "nm_done", "ex_done", "g3_done", "turned", "gates_done",
                 "z_ready", "relu_done", "hg_done", "acc_done", "ot_done", "stored", "bn_done"]
        S = {n: sem(n) for n in names}

        block = ctx.enter_context(nc.Block())

        class Steps:

            def __init__(self, eng, s):
                self.eng, self.s, self.n, self.per, self.base = eng, s, 0, 0, 0

            def start(self, b):
                if self.per == 0 and self.n:
                    self.per = self.n
                assert self.per == 0 or self.n == self.per
                self.n, self.base = 0, b * self.per

            def did(self, ins):
                ins.then_inc(self.s, 1)
                self.n += 1

            def wait(self):
                self.eng.wait_ge(self.s, self.base + self.n)

            def then(self, ins):
                self.did(ins)
                self.wait()

        def run(eng, ffn_pair, ffn_end, step):
            for name, _ in STEPS:
                step(name, 0)
            with eng.Fori(0, B - 1) as i:
                for p in range(NP):
                    if ffn_pair:
                        ffn_pair(i, p)
                    for name, at in STEPS:
                        if at == p:
                            step(name, i + 1)
                if ffn_end:
                    ffn_end(i)
            if ffn_pair:
                for p in range(NP):
                    ffn_pair(B - 1, p)
            if ffn_end:
                ffn_end(B - 1)

        @block.sync
        def _(eng):
            eng.dma_start(par[:], par_d).then_inc(ld_par, 16)
            eng.dma_start(ctxT[:], ctx_d).then_inc(ld_ctx, 16)
            eng.dma_start(small[:], small_d).then_inc(ld_par, 16)
            eng.dma_start(xr[:], xr_d).then_inc(ld_xr, 16)
            eng.dma_start(selbc[:], selbc_d).then_inc(ld_sel, 16)
            eng.dma_start(xT[:], xT_d).then_inc(ld_xT, 16)
            eng.dma_start(selg[:], selg_d).then_inc(ld_selg, 16)
            for i, s in enumerate(ld_w):
                a, e = i * WCH, min(NT, (i + 1) * WCH)
                eng.dma_start(wall[:, a:e, :], wall_d[:, a:e, :]).then_inc(s, 16)
            with eng.Fori(0, B) as i:
                eng.wait_ge(S["ot_done"], i + 2)
                eng.dma_start(out_d[:, :, i, :], ot[:]).then_inc(S["stored"], 16)
            eng.wait_ge(S["stored"], 16 * (B + 1))

        @block.tensor
        def _(pe):
            def step(name, b):
                if name == "xin":
                    if type(b) is int:
                        pe.wait_ge(ld_par, 32)
                        pe.wait_ge(ld_ctx, 16)
                    for k in range(KD):
                        mm = pe.matmul(misc[:, k, :], win[:, k * P:(k + 1) * P], ctxT[:, b, :], start=True, stop=True)
                    mm.then_inc(S["xin_done"], 1)
                elif name == "xdbl":
                    pe.wait_ge(S["u_done"], b + 1)
                    for k in range(KD):
                        pe.matmul(misc[0:96, 0, :], xbc[:, k, :], u[:, k, :], start=k == 0, stop=k == KD - 1)
                    for k in range(KD):
                        mm = pe.matmul(misc[0:DR, 1, :], xdt[:, k, :], u[:, k, :], start=k == 0, stop=k == KD - 1)
                    mm.then_inc(S["xdbl_done"], 1)
                elif name == "dt":
                    pe.wait_ge(S["dtl_done"], b + 1)
                    for k in range(KD):
                        mm = pe.matmul(misc[:, k, :], dtw[:, k * P:(k + 1) * P], dtl[:], start=True, stop=True)
                    mm.then_inc(S["dt_done"], 1)
                elif type(name) is tuple:
                    c = name[1]
                    if c == 0:
                        if type(b) is int:
                            pe.wait_ge(ld_sel, 16)
                        pe.wait_ge(S["bcs_done"], b + 1)
                    else:
                        pe.wait_ge(S["bu_done"], b * NC + c)
                    for j in range(2):
                        mm = pe.matmul(bb[:, j, :], selbc[:, 2 * c + j, :], bcs[:], start=True, stop=True)
                    mm.then_inc(S["b_ready"], 1)
                    if c:
                        pe.wait_ge(S["prod_done"], b * NC + c)
                    for j in range(2):
                        mm = pe.matmul(cc[:, j, :], selbc[:, NS + 2 * c + j, :], bcs[:], start=True, stop=True)
                    mm.then_inc(S["c_ready"], 1)
                elif name == "mean":
                    if type(b) is int:
                        pe.wait_ge(const_done, 3)
                    pe.wait_ge(S["x1_done"], b + 1)
                    for k in range(KD):
                        mm = pe.matmul(misc[:, 0, :], meanw[:], x1[:, b % 2, k, :], start=k == 0, stop=k == KD - 1)
                    mm.then_inc(S["mean_done"], 1)
                elif name == "var":
                    pe.wait_ge(S["sq_done"], b + 1)
                    for k in range(KD):
                        mm = pe.matmul(misc[:, 0, :], meanw[:], sq[:, k, :], start=k == 0, stop=k == KD - 1)
                    mm.then_inc(S["var_done"], 1)
                elif name == "logits":
                    pe.wait_ge(S["xs_done"], b + 1)
                    for t in range(2):
                        for k in range(KD):
                            mm = pe.matmul(misc[:, t, 0:NR], xs[:, k, t * P:(t + 1) * P], rw[:, k, :],
                                           start=k == 0, stop=k == KD - 1)
                    mm.then_inc(S["logits_done"], 1)
                elif name == "turn":
                    pe.wait_ge(S["g3_done"], b + 1)
                    for t in range(2):
                        pe.transpose(miscb[0:3 * NR, t * P:(t + 1) * P],
                                     g3[:, t].rearrange("p a b -> p (a b)"), identb[:])
                    for t in range(2):
                        mm = pe.transpose(misc[0:NR + NSH, 1, t * P:(t + 1) * P], g34[:, t, :], ident)
                    mm.then_inc(S["turned"], 1)

            def second_layer(b, p):
                pe.wait_ge(S["hg_done"], b * NP + p + 1)
                if p == 0:
                    pe.wait_ge(S["ot_done"], b + 1)
                    for k in range(KD):
                        pe.matmul(acc[:, k, :], b2x[:, k * P:(k + 1) * P], gT[:], start=k == 0, stop=False,
                                  skip_group_check=True)
                for t in range(2 * p, min(2 * p + 2, NT)):
                    for k in range(KD):
                        mm = pe.matmul(acc[:, k, :], wall[:, t, (2 + k) * P:(3 + k) * P], hg[:, p % 2, t % 2, :],
                                       start=False, stop=t == NT - 1, skip_group_check=True)
                if p == NP - 1:
                    mm.then_inc(S["acc_done"], 1)

            def pair(b, p):
                if p == 0:
                    pe.wait_ge(S["gates_done"], b + 1)
                    pe.wait_ge(S["xn_done"], b + 1)
                    pe.wait_ge(ld_selg, 16)
                for t in range(2 * p, min(2 * p + 2, NT)):
                    if t % WCH == 0:
                        pe.wait_ge(ld_w[t // WCH], 16)
                    for k in range(KD):
                        mm = pe.matmul(z[p % 2][:, t % 2, :], wall[:, t, k * P:(k + 1) * P], xn[:, b % 2, k, :],
                                       start=k == 0, stop=k == KD - 1)
                    if t < NT_R:
                        mm = pe.matmul(gb[p % 2][:, t % 2, :], selg[:, t, :], gst[:, b % 2, :], start=True, stop=True)
                mm.then_inc(S["z_ready"], 1)
                if p:
                    second_layer(b, p - 1)

            run(pe, pair, lambda b: second_layer(b, NP - 1), step)

        @block.scalar
        def _(act):
            me = Steps(act, act_step)
            act.preload_act_table_set("natural_log_exp_and_others")
            act.wait_ge(ld_par, 32)
            act.activation(aneg[:], pv("alog"), ACT.Exp).then_inc(aexp_done, 1)

            def step(name, b):
                if name == "xin":
                    me.start(b)
                    if type(b) is int:
                        act.wait_ge(var1_done, 1)
                        act.activation(t1[:], mv[:, :, :, 1:2], ACT.Ln, bias=epsc[:]).then_inc(ln1_done, 1)
                        act.wait_ge(ln1_done, 1)
                        act.activation(rs1[:], t1[:], ACT.Exp, scale=-0.5).then_inc(rstd1_done, 1)
                elif name == "conv":
                    act.wait_ge(S["conv_done"], b + 1)
                    act.activation(e1[:], cv[:], ACT.Exp, scale=-1.0).then_inc(S["econv_done"], 1)
                elif name == "delta":
                    act.wait_ge(S["v_done"], b + 1)
                    me.then(act.activation(sp[:], v[:], ACT.Abs))
                    me.then(act.activation(sp[:], sp[:], ACT.Exp, scale=-1.0))
                    act.activation(sp[:], sp[:], ACT.Ln, bias=1.0).then_inc(S["sp_done"], 1)
                elif name == "zgate":
                    act.wait_ge(S["zz_done"], b + 1)
                    act.activation(e1[:], zz[:], ACT.Exp, scale=-1.0).then_inc(S["ez_done"], 1)
                elif type(name) is tuple:
                    c = name[1]
                    if c == 0:
                        act.wait_ge(S["delta_done"], b + 1)
                        if type(b) is int:
                            act.wait_ge(aneg_done, 1)
                    for k in range(KD):
                        if c:
                            act.wait_ge(S["scan_done"], (b * NC + c - 1) * KD + k + 1)
                        for j in range(2):
                            n = k * NS + 2 * c + j
                            ins = act.activation(dA[:, k, j * L:(j + 1) * L], delta[:, k, :], ACT.Exp,
                                                 scale=aneg[:, n:n + 1])
                        ins.then_inc(S["da_ready"], 1)
                elif name == "centre":
                    act.wait_ge(S["xc_done"], b + 1)
                    act.activation(sq[:], xc[:], ACT.Square).then_inc(S["sq_done"], 1)
                elif name == "norm":
                    act.wait_ge(S["var_done"], b + 1)
                    me.then(act.activation(r2[:], misc[:, 0, :], ACT.Ln, bias=epsc[:]))
                    act.activation(r2[:], r2[:], ACT.Exp, scale=-0.5).then_inc(S["r2_done"], 1)
                elif name == "logits":
                    act.wait_ge(S["xs_done"], b + 1)
                    act.activation(xn[:, b % 2], xs[:], ACT.Copy).then_inc(S["xn_done"], 1)
                elif name == "gates":
                    act.wait_ge(S["nm_done"], b + 1)
                    for t in range(2):
                        ins = act.activation(ex[:, t, :], lg[:, t, 0:NR], ACT.Exp, bias=nm[:, t:t + 1])
                    ins.then_inc(S["ex_done"], 1)
                elif name == "turn":
                    act.wait_ge(S["turned"], b + 1)
                    act.activation(gst[:, b % 2, :], miscb[0:3 * NR, 0:L], ACT.Copy)
                    act.activation(gT[:], misc[0:NR + NSH, 1, :], ACT.Copy).then_inc(S["gates_done"], 1)

            def pair(b, p):
                act.wait_ge(S["z_ready"], b * NP + p + 1)
                for t in range(2 * p, min(2 * p + 2, NT)):
                    ins = act.activation(r[:, p % 2, t % 2, :], z[p % 2][:, t % 2, :], ACT.Relu, bias=b1[:, t:t + 1])
                ins.then_inc(S["relu_done"], 1)

            run(act, pair, None, step)

        @block.vector
        def _(dve):
            me = Steps(dve, dve_step)
            dve.memset(epsc[:], EPS).then_inc(const_done, 1)
            dve.memset(meanw[:], 1.0 / DX).then_inc(const_done, 1)
            dve.memset(lg[:], LOWEST).then_inc(S["ot_done"], 1)
            dve.memset(g34[:], 1.0 / NSH).then_inc(S["stored"], 16)
            dve.wait_ge(ld_par, 32)
            dve.tensor_copy(identb[:], ident).then_inc(const_done, 1)
            dve.wait_ge(aexp_done, 1)
            dve.tensor_scalar(aneg[:], aneg[:], -1.0, None, ALU.mult).then_inc(aneg_done, 1)

            def step(name, b):
                if name == "xin":
                    me.start(b)
                elif name == "conv":
                    dve.wait_ge(S["xin_done"], b + 1)
                    for k in range(KD):
                        me.did(dve.tensor_scalar(cv[:, k, :], misc[:, k, :], cw[:, k, KC - 1:KC], cb[:, k:k + 1],
                                                 ALU.mult, ALU.add))
                    for s in range(1, KC):
                        me.wait()
                        for k in range(KD):
                            ins = dve.scalar_tensor_tensor(cv[:, k, s:], misc[:, k, 0:L - s],
                                                           cw[:, k, KC - 1 - s:KC - s], cv[:, k, s:],
                                                           ALU.mult, ALU.add)
                            if s < KC - 1:
                                me.did(ins)
                    ins.then_inc(S["conv_done"], 1)
                    if type(b) is int:
                        dve.wait_ge(ld_xr, 16)
                        for n in range(KD * B):
                            ins = dve.bn_stats(st6[:, n, :], xr[:, n // B, n % B, :])
                        ins.then_inc(S["bn_done"], 1)
                        dve.wait_ge(S["bn_done"], 1)
                        for n in range(KD * B):
                            ins = dve.bn_aggr(mv[:, n // B, n % B, :], st6[:, n, :])
                        ins.then_inc(var1_done, 1)
                elif name == "u":
                    dve.wait_ge(S["econv_done"], b + 1)
                    me.then(dve.tensor_scalar(e1[:], e1[:], 1.0, None, ALU.add))
                    me.then(dve.reciprocal(rec[:], e1[:]))
                    dve.tensor_tensor(u[:], cv[:], rec[:], ALU.mult).then_inc(S["u_done"], 1)
                elif name == "split":
                    dve.wait_ge(S["xdbl_done"], b + 1)
                    me.did(dve.tensor_copy(bcx[:], misc[0:96, 0, :]))
                    dve.tensor_copy(dtl[:], misc[0:DR, 1, :]).then_inc(S["dtl_done"], 1)
                    me.wait()
                    me.then(dve.tensor_copy(bcs[:], bcx[:]))
                    me.then(dve.tensor_tensor(bcr[:], bcx[:], bcs[:], ALU.subtract))
                    me.then(dve.tensor_copy(bcm[:], bcr[:]))
                    dve.tensor_copy(bcs[32:64, :], bcm[32:64, :])
                    dve.tensor_tensor(bcs[64:96, :], bcr[64:96, :], bcm[64:96, :],
                                      ALU.subtract).then_inc(S["bcs_done"], 1)
                elif name == "delta":
                    dve.wait_ge(S["dt_done"], b + 1)
                    for k in range(KD):
                        ins = dve.tensor_scalar(v[:, k, :], misc[:, k, :], dtb[:, k:k + 1], None, ALU.add)
                    ins.then_inc(S["v_done"], 1)
                    dve.wait_ge(S["sp_done"], b + 1)
                    me.then(dve.scalar_tensor_tensor(delta[:], v[:], 0.0, sp[:], ALU.max, ALU.add))
                    dve.tensor_tensor(du[:], delta[:], u[:], ALU.mult).then_inc(S["delta_done"], 1)
                elif name == "zgate":
                    if type(b) is int:
                        dve.wait_ge(rstd1_done, 1)
                    for k in range(KD):
                        ins = dve.tensor_scalar(zz[:, k, :], xr[:, k, b, :], mv[:, k, b, 0:1], rs1[:, k, b, :],
                                                ALU.subtract, ALU.mult)
                    ins.then_inc(S["zz_done"], 1)
                    dve.wait_ge(S["ez_done"], b + 1)
                    me.then(dve.tensor_scalar(e1[:], e1[:], 1.0, None, ALU.add))
                    me.then(dve.reciprocal(rec[:], e1[:]))
                    me.did(dve.tensor_tensor(sz[:], zz[:], rec[:], ALU.mult))
                elif type(name) is tuple:
                    c = name[1]
                    g = b * NC + c
                    if c:
                        dve.wait_ge(S["prod_done"], g)
                    dve.wait_ge(S["b_ready"], g + 1)
                    for k in range(KD):
                        ins = dve.tensor_tensor(bu[:, k, :].rearrange("p (j l) -> p j l", j=2), bb[:],
                                                du[:, k:k + 1, :].broadcast_to([P, 2, L]), ALU.mult)
                    ins.then_inc(S["bu_done"], 1)
                    dve.wait_ge(S["bu_done"], g + 1)
                    for k in range(KD):
                        dve.wait_ge(S["da_ready"], g * KD + k + 1)
                        for j in range(2):
                            one = slice(j * L, (j + 1) * L)
                            ins = dve.tensor_tensor_scan(bu[:, k, one], dA[:, k, one], bu[:, k, one], 0.0, ALU.mult,
                                                         ALU.add)
                        ins.then_inc(S["scan_done"], 1)
                    dve.wait_ge(S["c_ready"], g + 1)
                    for k in range(KD):
                        dve.wait_ge(S["scan_done"], g * KD + k + 1)
                        if c > 1:
                            dve.wait_ge(S["y_folded"], (b * NC + c - 2) * KD + k + 1 )
                        dst = ya if c == 0 else pr
                        ins = dve.tensor_tensor(dst[:, k, :], bu[:, k, :], cc[:].rearrange("p a b -> p (a b)"), ALU.mult)
                    ins.then_inc(S["prod_done"], 1)
                elif name == "x1":
                    dve.wait_ge(S["y_folded"], (b + 1) * NC * KD)
                    if type(b) is int:
                        dve.wait_ge(ld_xT, 16)
                    for k in range(KD):
                        me.did(dve.scalar_tensor_tensor(y[:, k, :], u[:, k, :], dd[:, k:k + 1], y[:, k, :], ALU.mult,
                                                        ALU.add))
                    me.wait()
                    me.then(dve.tensor_tensor(y[:], y[:], sz[:], ALU.mult))
                    dve.tensor_tensor(x1[:, b % 2], y[:], xT[:, :, b, :], ALU.add).then_inc(S["x1_done"], 1)
                elif name == "centre":
                    dve.wait_ge(S["mean_done"], b + 1)
                    dve.tensor_tensor(xc[:], x1[:, b % 2], misc[:, 0:1, :].broadcast_to([P, KD, L]),
                                      ALU.subtract).then_inc(S["xc_done"], 1)
                elif name == "norm":
                    dve.wait_ge(S["r2_done"], b + 1)
                    me.then(dve.scalar_tensor_tensor(n1[:], misc[:, 0, :], EPS, r2[:], ALU.add, ALU.mult))
                    me.then(dve.tensor_tensor(n2[:], n1[:], r2[:], ALU.mult))
                    me.then(dve.tensor_scalar(n1[:], n2[:], -0.5, 1.5, ALU.mult, ALU.add))
                    me.then(dve.tensor_tensor(n2[:], n1[:], r2[:], ALU.mult))
                    dve.tensor_tensor(xs[:], xc[:], n2[:].rearrange("p (o l) -> p o l", o=1)
                                      .broadcast_to([P, KD, L]), ALU.mult).then_inc(S["xs_done"], 1)
                elif name == "gates":
                    dve.wait_ge(S["logits_done"], b + 1)
                    me.then(dve.tensor_tensor(lg[:, :, 0:NR], misc[:, :, 0:NR],
                                              rb.rearrange("p (o n) -> p o n", o=1).broadcast_to([P, 2, NR]), ALU.add))
                    dve.memset(sink[:], 0.0)
                    for t in range(2):
                        me.did(dve.max(m8[:, t, :], lg[:, t, 0:NR]))
                    me.wait()
                    dve.tensor_scalar(nm[:], m8[:, :, 0], -1.0, None, ALU.mult).then_inc(S["nm_done"], 1)
                    me.then(dve.memset(m8[:, :, TOPK:8], LOWEST))
                    dve.memset(sink[:], 0.0)
                    for t in range(2):
                        me.did(dve.match_replace(rep[:, t, :], m8[:, t, :], lg[:, t, :], HUGE))
                    me.wait()
                    me.then(dve.tensor_tensor(mask[:], rep[:, :, 0:NR], lg[:, :, 0:NR], ALU.not_equal))
                    dve.wait_ge(S["ex_done"], b + 1)
                    me.then(dve.tensor_tensor(em[:], ex[:], mask[:], ALU.mult))
                    me.then(dve.tensor_reduce(sm[:], em[:], AX.X, ALU.add))
                    me.then(dve.reciprocal(rsm[:], sm[:]))
                    for t in range(2):
                        me.did(dve.tensor_scalar(g34[:, t, 0:NR], em[:, t, :], rsm[:, t:t + 1], None, ALU.mult))
                    me.wait()
                    me.then(dve.tensor_copy(g3[:, :, 0, :], g34[:, :, 0:NR]))
                    me.then(dve.tensor_tensor(gr[:], g34[:, :, 0:NR], g3[:, :, 0, :], ALU.subtract))
                    me.then(dve.tensor_copy(g3[:, :, 1, :], gr[:]))
                    dve.tensor_tensor(g3[:, :, 2, :], gr[:], g3[:, :, 1, :], ALU.subtract).then_inc(S["g3_done"], 1)

            def pair(b, p):
                dve.wait_ge(S["relu_done"], b * NP + p + 1)
                if 2 * p < NT_R:
                    ins = dve.tensor_tensor(hg[:, p % 2], r[:, p % 2], gb[p % 2][:], ALU.mult)
                else:
                    n = min(2, NT - 2 * p)
                    ins = dve.tensor_scalar(hg[:, p % 2, 0:n], r[:, p % 2, 0:n], 1.0 / NSH, None, ALU.mult)
                ins.then_inc(S["hg_done"], 1)

            def end(b):
                dve.wait_ge(S["acc_done"], b + 1)
                dve.wait_ge(S["stored"], b * 16 + 16)
                dve.tensor_tensor(ot[:], acc[:], x1[:, b % 2], ALU.add).then_inc(S["ot_done"], 1)

            run(dve, pair, end, step)

        @block.gpsimd
        def _(pool):
            def step(name, b):
                if type(name) is tuple:
                    c = name[1]
                    if c == 0:
                        return
                    pool.wait_ge(S["prod_done"], b * NC + c + 1)
                    for k in range(KD):
                        if c > 1 :
                            pool.wait_ge(S["y_folded"], (b * NC + c - 2) * KD + k + 1)
                        pool.tensor_tensor(ya[:, k, :], ya[:, k, :], pr[:, k, :], ALU.add).then_inc(S["y_folded"], 1)
                elif name == "x1":
                    for k in range(KD):
                        pool.wait_ge(S["y_folded"], (b * NC + NC - 2) * KD + k + 1)
                        pool.tensor_tensor(y[:, k, :], ya[:, k, 0:L], ya[:, k, L:2 * L], ALU.add).then_inc(S["y_folded"], 1)

            run(pool, None, None, step)


def kernel(**inputs):
    import ml_dtypes
    import numpy as np
    import concourse.bacc as bacc
    from concourse.bass_utils import run_bass_kernel_spmd

    def get(n):
        return np.asarray(inputs[n])

    def halves(a):
        return a.reshape((KD, P) + a.shape[1:]).swapaxes(0, 1)

    x = get("x")
    xa = {k: get("L0_xattn_" + k) for k in ("in_proj_w", "conv_w", "conv_b", "x_proj_w", "dt_proj_w", "dt_proj_b",
                                            "A_log", "D")}
    ff = {k: get("L0_ffn_" + k) for k in ("sw1", "sb1", "sw2", "sb2", "rw1", "rb1", "rw2", "rb2", "router_w",
                                          "router_b")}
    f32 = x.dtype
    nh = (NR + NSH) * HID
    w1 = np.zeros((DX, NT * P), f32)
    w1[:, :NR * HID] = ff["rw1"].transpose(1, 0, 2).reshape(DX, -1)
    w1[:, NR * HID:nh] = ff["sw1"].transpose(1, 0, 2).reshape(DX, -1)
    w2 = np.zeros((NT * P, DX), f32)
    w2[:NR * HID] = ff["rw2"].reshape(-1, DX)
    w2[NR * HID:nh] = ff["sw2"].reshape(-1, DX)
    b1 = np.zeros((NT * P,), f32)
    b1[:NR * HID] = ff["rb1"].reshape(-1)
    b1[NR * HID:nh] = ff["sb1"].reshape(-1)
    wall = np.concatenate([w1.reshape(KD, P, NT, P).transpose(1, 2, 0, 3).reshape(P, NT, KD * P),
                           w2.reshape(NT, P, DX).transpose(1, 0, 2)], axis=2)
    xp = halves(xa["x_proj_w"].T)
    par = np.zeros((P, NPAR), f32)

    def put(name, a):
        par[:, PAR[name][0]:PAR[name][1]] = a.reshape(P, -1)

    put("win", xa["in_proj_w"].T)
    put("xbc", np.concatenate([xp[:, :, DR:]] * 3, axis=2))
    put("xdt", xp[:, :, :DR])
    put("cw", halves(xa["conv_w"]))
    put("cb", halves(xa["conv_b"]))
    put("dtb", halves(xa["dt_proj_b"]))
    put("alog", halves(xa["A_log"]))
    put("dd", halves(xa["D"]))
    put("rw", halves(ff["router_w"]))
    put("rb", np.broadcast_to(ff["router_b"], (P, NR)))
    put("b1", b1.reshape(NT, P).T)
    put("ident", np.eye(P, dtype=f32))
    small = np.zeros((NR + NSH, 2 * DX), f32)
    small[:DR, :DX] = xa["dt_proj_w"].T
    small[:NR, DX:] = ff["rb2"]
    small[NR:, DX:] = ff["sb2"]
    expert = np.arange(NR * HID) // HID
    selg = np.tile((expert[None, :] == np.arange(NR)[:, None]), (3, 1)).astype(ml_dtypes.bfloat16)
    selbc = np.tile(np.eye(2 * NS), (3, 1)).astype(ml_dtypes.bfloat16)
    selbc = np.repeat(selbc[:, :, None], P, axis=2)
    arrays = {
        "in_xT": halves(x.transpose(2, 0, 1)),
        "in_xr": halves(x.transpose(1, 0, 2)),
        "in_ctx": get("ctx_1024").transpose(2, 0, 1),
        "in_par": par,
        "in_small": small,
        "in_wall": wall,
        "in_selg": selg.reshape(3 * NR, NT_R, P),
        "in_selbc": selbc,
    }
    arrays = {k: np.ascontiguousarray(a) for k, a in arrays.items()}
    nc = bacc.Bacc("TRN2", target_bir_lowering=False, num_devices=1)
    args = [nc.dram_tensor(k, a.shape, mybir.dt.from_np(a.dtype), kind="ExternalInput").ap() for k, a in arrays.items()]
    out = nc.dram_tensor("out_0", (P, KD, B, L), F32, kind="ExternalOutput").ap()
    xattn_ffn_kernel(nc, *args, out)
    r = run_bass_kernel_spmd(nc, [arrays], core_ids=[0])
    o = r.results[0]["out_0"]
    return np.ascontiguousarray(o.transpose(2, 3, 1, 0).reshape(B, L, DX))
```

```python
from contextlib import ExitStack

import concourse.bass as bass
from concourse import mybir

F32 = mybir.dt.float32
F32R = mybir.dt.float32r
BF16 = mybir.dt.bfloat16
ALU = mybir.AluOpType
ACT = mybir.ActivationFunctionType
AX = mybir.AxisListType

P = 128
B, L, DX = 4, 256, 256
DC_IN = 128
KD = DX // P
NS, DR, KC = 16, 8, 4
NR, NSH, HID, TOPK = 32, 2, 176, 6
NT_S = -(-NSH * HID // P)
NT_R = NR * HID // P
NT = NT_S + NT_R
PAIRS = [[0, 1], [2]] + [[t, t + 1] for t in range(NT_S, NT, 2)]
NP = len(PAIRS)
NC = NS // 2
EPS = 1e-5
LOWEST = -3.0e38
HUGE = 3.0e38
WCH = 4
NW = -(-NT // WCH)

PAR = {}
_at = 0
for _name, _n in (("win", DX), ("xbc", KD * 3 * 2 * NS), ("xdt", KD * DR), ("cw", KD * KC), ("cb", KD), ("dtb", KD),
                  ("alog", KD * NS), ("dd", KD), ("rw", KD * NR), ("rb", NR), ("b1", NT), ("ident", P)):
    PAR[_name] = (_at, _at + _n)
    _at += _n
NPAR = _at

STEPS = [("xin", 0), ("conv", 0), ("u", 1), ("xdbl", 2), ("split", 2), ("dt", 3), ("stats", 3), ("delta", 4)]
STEPS += [(("chunk", c), 5 + (c * 14) // 8) for c in range(NC)]
STEPS.insert([n for n, _ in STEPS].index(("chunk", 3)), ("zgate", 9))
STEPS += [("x1", 19), ("mean", 20), ("centre", 20), ("var", 21), ("norm", 21), ("logits", 22)]
OWN_STEPS = [("gates", 0), ("turn", 1)]


def xattn_ffn_kernel(nc: bass.Bass, xT_d, xr_d, ctx_d, par_d, small_d, w1_d, w2_d, selg_d, selbc_d, out_d):
    ctx = ExitStack()
    with ctx:
        def sb(name, shape, dt=F32):
            return ctx.enter_context(nc.sbuf_tensor(name, shape, dt))

        def ps(name, shape, dt=F32):
            return ctx.enter_context(nc.psum_tensor(name, shape, dt))

        def sem(name):
            return ctx.enter_context(nc.semaphore(name))

        xT = sb("xT", [P, KD, L])
        xr = sb("xr", [P, KD, DX])
        ctxT = sb("ctxT", [P, B, L])
        par = sb("par", [P, NPAR])
        small = sb("small", [NR + NSH, 2 * DX])
        w1h = sb("w1h", [P, NT, KD * P], F32R)
        w1l = sb("w1l", [P, NT, KD * P], F32R)
        w2 = sb("w2", [P, NT, DX])
        selg = sb("selg", [3 * NR, NT_R, P], BF16)
        selbc = sb("selbc", [3 * 2 * NS, 2 * NS], BF16)

        def pv(name):
            return par[:, PAR[name][0]:PAR[name][1]]

        win, cb, dtb, dd, rb, b1, ident = (pv(n) for n in ("win", "cb", "dtb", "dd", "rb", "b1", "ident"))
        xbc = pv("xbc").rearrange("p (k m) -> p k m", k=KD)
        xdt = pv("xdt").rearrange("p (k m) -> p k m", k=KD)
        cw = pv("cw").rearrange("p (k m) -> p k m", k=KD)
        rw = pv("rw").rearrange("p (k m) -> p k m", k=KD)
        dtw = small[0:DR, 0:DX]
        b2x = small[:, DX:2 * DX]

        identb = sb("identb", [P, P], BF16)
        meanw = sb("meanw", [P, P])
        aneg = sb("aneg", [P, KD * NS])
        epsc = sb("epsc", [P, 1])
        st6 = sb("st6", [P, KD, 6])
        mv = sb("mv", [P, KD, 2])
        rs1 = sb("rs1", [P, KD])
        nb1 = sb("nb1", [P, KD])
        cv = sb("cv", [P, KD, L])
        e1 = sb("e1", [P, KD, L])
        rec = sb("rec", [P, KD, L])
        u = sb("u", [P, KD, L])
        bcs = sb("bcs", [96, L], BF16)
        delta = sb("delta", [P, KD, L])
        du = sb("du", [P, KD, L])
        sz = sb("sz", [P, KD, L])
        dA = sb("dA", [P, KD, 2 * L])
        bu = sb("bu", [P, KD, 2 * L])
        pr = sb("pr", [P, KD, 2 * L])
        ya = sb("ya", [P, KD, 2 * L])
        x1 = sb("x1", [P, 2, KD, L])
        bcr, bcm, dtl = e1[0:96, 0, :], e1[0:96, 1, 0:L // 2].bitcast(BF16), rec[0:DR, 0, :]
        v, sp, zz = rec, e1, cv
        y = pr[:, :, 0:L]
        xc, sq, xs = e1, y, delta
        r2, n1, n2 = cv[:, 0, :], cv[:, 1, :], rec[:, 0, :]
        xh = sb("xh", [P, 2, KD, L], F32R)
        xl = sb("xl", [P, 2, KD, L], F32R)
        lg = sb("lg", [P, 2, NR + 2])
        m8 = sb("m8", [P, 2, 8])
        nm = sb("nm", [P, 2])
        sink = sb("sink", [P, 1])
        rep = sb("rep", [P, 2, NR + 2])
        ex = sb("ex", [P, 2, NR])
        mask = sb("mask", [P, 2, NR])
        em = sb("em", [P, 2, NR])
        sm = sb("sm", [P, 2])
        rsm = sb("rsm", [P, 2])
        g34 = sb("g34", [P, 2, NR + NSH])
        gr = sb("gr", [P, 2, NR])
        g3 = sb("g3", [P, 2, 3, NR], BF16)
        gst = sb("gst", [3 * NR, L], BF16)
        gT = sb("gT", [NR + NSH, L])
        stage = sb("stage", [P, 2, WCH * KD * P])
        r = stage[:, 0, :].rearrange("p (a b l) -> p a b l", a=2, b=2)
        hg = stage[:, 1, :].rearrange("p (a b l) -> p a b l", a=2, b=2)

        z = [ps(f"z{i}", [P, 2, L]) for i in range(2)]
        gb = [ps(f"gb{i}", [P, 2, L]) for i in range(2)]
        acc = ps("acc", [P, KD, L])
        bb = ps("bb", [P, 2, L])
        cc = ps("cc", [P, 2, L])
        misc = ps("misc", [P, 2, L])
        miscb = misc[:].rearrange("p a b -> p (a b)").bitcast(BF16)

        ld_ctx, ld_par, ld_xr, ld_xT, ld_sel, ld_selg = (sem(n) for n in
                                                         ("ld_ctx", "ld_par", "ld_xr", "ld_xT", "ld_sel", "ld_selg"))
        ld_w1 = [sem(f"ld_w1_{i}") for i in range(2)]
        ld_w2 = [sem(f"ld_w2_{i}") for i in range(NW)]
        w1h_done, w1l_done = sem("w1h_done"), sem("w1l_done")
        dve_step, dve_router_step, act_step = sem("dve_step"), sem("dve_router_step"), sem("act_step")
        aexp_done, aneg_done, const_done = sem("aexp_done"), sem("aneg_done"), sem("const_done")
        names = ["xin_done", "conv_done", "econv_done", "u_done", "dtlo_done", "xdbl_done", "dtl_done", "bcs_done", "dt_done",
                 "v_done", "sp_done", "delta_done", "zz_done", "ez_done", "b_ready", "c_ready", "bu_done", "da_ready",
                 "scan_done", "prod_done", "y_folded", "x1_done", "xs_done", "mean_done", "xc_done", "sq_done", "var_done", "r2_done",
                 "xh_done", "xl_done", "logits_done", "nm_done", "ex_done", "g3_done", "turned", "gates_done",
                 "z_ready", "relu_done", "hg_done", "acc_done", "ot_done", "stored", "aggr_done", "rs1_done", "nb1_done",
                 "cv0_done", "bc0_done", "y_added"]
        S = {n: sem(n) for n in names}

        block = ctx.enter_context(nc.Block())

        class Steps:

            def __init__(self, eng, s, per):
                self.eng, self.s, self.n, self.per, self.base = eng, s, per, per, 0

            def start(self, b):
                assert self.n == self.per, self.n
                self.n, self.base = 0, b * self.per

            def did(self, ins):
                ins.then_inc(self.s, 1)
                self.n += 1

            def wait(self):
                self.eng.wait_ge(self.s, self.base + self.n)

            def then(self, ins):
                self.did(ins)
                self.wait()

        def run(eng, ffn_pair, ffn_end, step):
            for name, _ in STEPS:
                step(name, 0)
            with eng.Fori(0, B - 1) as i:
                for p in range(NP):
                    ffn_pair(i, p)
                    for name, at in OWN_STEPS:
                        if at == p:
                            step(name, i)
                    for name, at in STEPS:
                        if at == p:
                            step(name, i + 1)
                ffn_end(i)
            for p in range(NP):
                ffn_pair(B - 1, p)
                for name, at in OWN_STEPS:
                    if at == p:
                        step(name, B - 1)
            ffn_end(B - 1)

        def nothing(*_):
            pass

        def first(name, b):
            return type(b) is int and b == 0

        @block.sync
        def _(eng):
            eng.dma_start(par[:], par_d).then_inc(ld_par, 16)
            eng.dma_start(ctxT[:], ctx_d).then_inc(ld_ctx, 16)
            eng.dma_start(small[:], small_d).then_inc(ld_par, 16)
            eng.dma_start(xr[:], xr_d[:, :, 0, :]).then_inc(ld_xr, 16)
            eng.dma_start(selbc[:], selbc_d).then_inc(ld_sel, 16)
            eng.dma_start(xT[:], xT_d[:, :, 0, :]).then_inc(ld_xT, 16)
            for i in range(NW):
                a, e = i * WCH, min(NT, (i + 1) * WCH)
                if i >= 2:
                    eng.wait_ge(w1l_done, i - 1)
                eng.dma_start(stage[:, i % 2, 0:(e - a) * KD * P].rearrange("p (t m) -> p t m", m=KD * P),
                              w1_d[:, a:e, :]).then_inc(ld_w1[i % 2], 16)
                eng.dma_start(w2[:, a:e, :], w2_d[:, a:e, :]).then_inc(ld_w2[i], 16)
                if i == 1:
                    eng.dma_start(selg[:], selg_d).then_inc(ld_selg, 16)

            def store(b):
                eng.wait_ge(S["ot_done"], b + 2)
                eng.dma_start(out_d[:, :, b, :], x1[:, b % 2]).then_inc(S["stored"], 16)

            with eng.Fori(0, B - 1) as i:
                eng.wait_ge(S["zz_done"], i + 1)
                eng.dma_start(xr[:], xr_d[:, :, i + 1, :]).then_inc(ld_xr, 16)
                eng.wait_ge(S["x1_done"], i + 1)
                eng.dma_start(xT[:], xT_d[:, :, i + 1, :]).then_inc(ld_xT, 16)
                store(i)
            store(B - 1)
            eng.wait_ge(S["stored"], 16 * (B + 1))

        @block.tensor
        def _(pe):
            def sum_states(c):
                for k in range(KD):
                    for j in range(2):
                        if k + j == 0:
                            pe.wait_ge(S["prod_done"], c + 1)
                        mm = pe.matmul(acc[:, k, :], ident, pr[:, k, j * L:(j + 1) * L], start=c + k + j == 0,
                                       stop=c == NC - 1 and j == 1, skip_group_check=True)
                mm.then_inc(S["y_added"], 1)

            def step(name, b):
                if name == "xin":
                    if type(b) is int:
                        pe.wait_ge(ld_par, 32)
                        pe.wait_ge(ld_ctx, 16)
                    for k in range(KD):
                        mm = pe.matmul(bb[:, k, :], win[:, k * P:(k + 1) * P], ctxT[:, b, :], start=True, stop=True)
                    mm.then_inc(S["xin_done"], 1)
                elif name == "xdbl":
                    pe.wait_ge(S["u_done"], b + 1)
                    for k in range(KD):
                        mm = pe.matmul(cc[0:DR, 0, :], xdt[:, k, :], u[:, k, :], start=k == 0, stop=k == KD - 1)
                    mm.then_inc(S["dtlo_done"], 1)
                    for k in range(KD):
                        mm = pe.matmul(misc[0:96, 0, :], xbc[:, k, :], u[:, k, :], start=k == 0, stop=k == KD - 1)
                    mm.then_inc(S["xdbl_done"], 1)
                elif name == "dt":
                    pe.wait_ge(S["dtl_done"], b + 1)
                    for k in range(KD):
                        mm = pe.matmul(bb[:, k, :], dtw[:, k * P:(k + 1) * P], dtl, start=True, stop=True)
                    mm.then_inc(S["dt_done"], 1)
                elif type(name) is tuple:
                    c = name[1]
                    if c == 0:
                        if type(b) is int:
                            pe.wait_ge(ld_sel, 16)
                        pe.wait_ge(S["bcs_done"], b + 1)
                        pe.wait_ge(S["sp_done"], b + 1)
                    else:
                        pe.wait_ge(S["bu_done"], b * NC + c)
                    for j in range(2):
                        mm = pe.matmul(bb[:, j, :], selbc[:, 2 * c + j:2 * c + j + 1].broadcast_to([96, P]), bcs[:],
                                       start=True, stop=True)
                    mm.then_inc(S["b_ready"], 1)
                    if c:
                        pe.wait_ge(S["prod_done"], b * NC + c)
                    for j in range(2):
                        n = NS + 2 * c + j
                        mm = pe.matmul(cc[:, j, :], selbc[:, n:n + 1].broadcast_to([96, P]), bcs[:],
                                       start=True, stop=True)
                    mm.then_inc(S["c_ready"], 1)
                    if first(name, b):
                        if c:
                            sum_states(c - 1)
                        if c == NC - 1:
                            sum_states(c)
                elif name == "mean":
                    if type(b) is int:
                        pe.wait_ge(const_done, 3)
                    pe.wait_ge(S["x1_done"], b + 1)
                    for k in range(KD):
                        mm = pe.matmul(misc[:, 0, :], meanw[:], x1[:, b % 2, k, :], start=k == 0, stop=k == KD - 1)
                    mm.then_inc(S["mean_done"], 1)
                elif name == "var":
                    pe.wait_ge(S["sq_done"], b + 1)
                    for k in range(KD):
                        mm = pe.matmul(misc[:, 0, :], meanw[:], sq[:, k, :], start=k == 0, stop=k == KD - 1)
                    mm.then_inc(S["var_done"], 1)
                elif name == "logits":
                    pe.wait_ge(S["xs_done"], b + 1)
                    for t in range(2):
                        for k in range(KD):
                            mm = pe.matmul(misc[:, t, 0:NR], xs[:, k, t * P:(t + 1) * P], rw[:, k, :],
                                           start=k == 0, stop=k == KD - 1)
                    mm.then_inc(S["logits_done"], 1)
                elif name == "turn":
                    pe.wait_ge(S["g3_done"], b + 1)
                    for t in range(2):
                        pe.transpose(miscb[0:3 * NR, t * P:(t + 1) * P],
                                     g3[:, t].rearrange("p a b -> p (a b)"), identb[:])
                    for t in range(2):
                        mm = pe.transpose(misc[0:NR + NSH, 1, t * P:(t + 1) * P], g34[:, t, :], ident)
                    mm.then_inc(S["turned"], 1)

            def second_layer(b, p):
                pe.wait_ge(S["hg_done"], b * NP + p + 1)
                if p == 0:
                    pe.wait_ge(S["ot_done"], b + 1)
                for i, t in enumerate(PAIRS[p]):
                    if t % WCH == 0:
                        pe.wait_ge(ld_w2[t // WCH], 16)
                    for k in range(KD):
                        mm = pe.matmul(acc[:, k, :], w2[:, t, k * P:(k + 1) * P], hg[:, p % 2, i, :],
                                       start=t + k == 0, stop=False, skip_group_check=True)
                if p == NP - 1:
                    for k in range(KD):
                        mm = pe.matmul(acc[:, k, :], b2x[:, k * P:(k + 1) * P], gT[:], start=False, stop=True,
                                       skip_group_check=True)
                    mm.then_inc(S["acc_done"], 1)

            def pair(b, p):
                if p == 0:
                    pe.wait_ge(S["xl_done"], b + 1)
                if p == 2:
                    pe.wait_ge(ld_selg, 16)
                    pe.wait_ge(S["gates_done"], b + 1)
                for i, t in enumerate(PAIRS[p]):
                    if t % WCH == 0:
                        pe.wait_ge(w1l_done, t // WCH + 1)
                    for k in range(KD):
                        one = slice(k * P, (k + 1) * P)
                        xh_, xl_ = xh[:, b % 2, k, :], xl[:, b % 2, k, :]
                        pe.matmul(z[p % 2][:, i, :], w1l[:, t, one], xh_, start=k == 0, stop=False)
                        pe.matmul(z[p % 2][:, i, :], w1h[:, t, one], xl_, start=False, stop=False)
                        mm = pe.matmul(z[p % 2][:, i, :], w1h[:, t, one], xh_, start=False, stop=k == KD - 1)
                    if t >= NT_S:
                        mm = pe.matmul(gb[p % 2][:, i, :], selg[:, t - NT_S, :], gst[:], start=True, stop=True)
                mm.then_inc(S["z_ready"], 1)
                if p:
                    second_layer(b, p - 1)

            run(pe, pair, lambda b: second_layer(b, NP - 1), step)

        @block.scalar
        def _(act):
            me = Steps(act, act_step, 4)
            act.preload_act_table_set("natural_log_exp_and_others")
            act.wait_ge(ld_par, 32)
            act.activation(aneg[:], pv("alog"), ACT.Exp).then_inc(aexp_done, 1)
            todo = list(range(NW))

            def split_w1(n):
                for i in todo[:n]:
                    a, e = i * WCH, min(NT, (i + 1) * WCH)
                    act.wait_ge(ld_w1[i % 2], 16 * (i // 2 + 1))
                    act.activation(w1h[:, a:e, :].rearrange("p t m -> p (t m)"), stage[:, i % 2, 0:(e - a) * KD * P],
                                   ACT.Copy).then_inc(w1h_done, 1)
                del todo[:n]

            def step(name, b):
                if name == "xin":
                    me.start(b)
                elif name == "conv":
                    act.wait_ge(S["xin_done"], b + 1)
                    for k in range(KD):
                        ins = act.activation(cv[:, k, :], bb[:, k, :], ACT.Identity, scale=cw[:, k, KC - 1:KC],
                                             bias=cb[:, k:k + 1])
                    ins.then_inc(S["cv0_done"], 1)
                    act.wait_ge(S["conv_done"], b + 1)
                    act.activation(e1[:], cv[:], ACT.Exp, scale=-1.0).then_inc(S["econv_done"], 1)
                elif name == "split":
                    act.wait_ge(S["dtlo_done"], b + 1)
                    act.activation(dtl, cc[0:DR, 0, :], ACT.Copy).then_inc(S["dtl_done"], 1)
                    act.wait_ge(S["xdbl_done"], b + 1)
                    act.activation(bcs[:], misc[0:96, 0, :], ACT.Copy).then_inc(S["bc0_done"], 1)
                elif name == "stats":
                    act.wait_ge(S["aggr_done"], b + 1)
                    me.then(act.activation(rs1[:], mv[:, :, 1], ACT.Ln, bias=epsc[:]))
                    act.activation(rs1[:], rs1[:], ACT.Exp, scale=-0.5).then_inc(S["rs1_done"], 1)
                elif name == "delta":
                    act.wait_ge(S["dt_done"], b + 1)
                    for k in range(KD):
                        ins = act.activation(sp[:, k, :], bb[:, k, :], ACT.Abs, bias=dtb[:, k:k + 1])
                    me.then(ins)
                    me.did(act.activation(sp[:], sp[:], ACT.Exp, scale=-1.0))
                    for k in range(KD):
                        act.activation(v[:, k, :], bb[:, k, :], ACT.Relu, bias=dtb[:, k:k + 1])
                    me.wait()
                    act.activation(sp[:], sp[:], ACT.Ln, bias=1.0).then_inc(S["sp_done"], 1)
                elif name == "zgate":
                    act.wait_ge(S["nb1_done"], b + 1)
                    for k in range(KD):
                        ins = act.activation(zz[:, k, :], xr[:, k, :], ACT.Identity, scale=rs1[:, k:k + 1],
                                             bias=nb1[:, k:k + 1])
                    ins.then_inc(S["zz_done"], 1)
                    act.wait_ge(S["zz_done"], b + 1)
                    act.activation(e1[:], zz[:], ACT.Exp, scale=-1.0).then_inc(S["ez_done"], 1)
                elif type(name) is tuple:
                    c = name[1]
                    if c == 0:
                        act.wait_ge(S["delta_done"], b + 1)
                        if first(name, b):
                            act.wait_ge(aneg_done, 1)
                    for k in range(KD):
                        if c:
                            act.wait_ge(S["scan_done"], (b * NC + c - 1) * KD + k + 1)
                        for j in range(2):
                            n = k * NS + 2 * c + j
                            ins = act.activation(dA[:, k, j * L:(j + 1) * L], delta[:, k, :], ACT.Exp,
                                                 scale=aneg[:, n:n + 1])
                        ins.then_inc(S["da_ready"], 1)
                    if first(name, b):
                        split_w1(2)
                elif name == "centre":
                    act.wait_ge(S["xc_done"], b + 1)
                    act.activation(sq, xc[:], ACT.Square).then_inc(S["sq_done"], 1)
                elif name == "norm":
                    act.wait_ge(S["var_done"], b + 1)
                    me.then(act.activation(r2, misc[:, 0, :], ACT.Ln, bias=epsc[:]))
                    act.activation(r2, r2, ACT.Exp, scale=-0.5).then_inc(S["r2_done"], 1)
                    act.wait_ge(S["xs_done"], b + 1)
                    act.activation(xh[:, b % 2], xs[:], ACT.Copy).then_inc(S["xh_done"], 1)
                elif name == "gates":
                    act.wait_ge(S["nm_done"], b + 1)
                    for t in range(2):
                        ins = act.activation(ex[:, t, :], lg[:, t, 0:NR], ACT.Exp, bias=nm[:, t:t + 1])
                    ins.then_inc(S["ex_done"], 1)
                elif name == "turn":
                    act.wait_ge(S["turned"], b + 1)
                    act.activation(gst[:], miscb[0:3 * NR, 0:L], ACT.Copy)
                    act.activation(gT[:], misc[0:NR + NSH, 1, :], ACT.Copy).then_inc(S["gates_done"], 1)

            def pair(b, p):
                if first("pair", b) or p == 0:
                    act.wait_ge(w1l_done, NW)
                act.wait_ge(S["z_ready"], b * NP + p + 1)
                for i, t in enumerate(PAIRS[p]):
                    ins = act.activation(r[:, p % 2, i, :], z[p % 2][:, i, :], ACT.Relu, bias=b1[:, t:t + 1])
                ins.then_inc(S["relu_done"], 1)

            run(act, pair, nothing, step)

        @block.vector
        def _(dve):
            me, own = Steps(dve, dve_step, 21), Steps(dve, dve_router_step, 15)
            dve.memset(epsc[:], EPS).then_inc(const_done, 1)
            dve.memset(meanw[:], 1.0 / DX).then_inc(const_done, 1)
            dve.memset(lg[:], LOWEST).then_inc(S["ot_done"], 1)
            dve.memset(g34[:], 1.0 / NSH).then_inc(S["stored"], 16)
            dve.wait_ge(ld_par, 32)
            dve.tensor_copy(identb[:], ident).then_inc(const_done, 1)
            dve.wait_ge(aexp_done, 1)
            dve.tensor_scalar(aneg[:], aneg[:], -1.0, None, ALU.mult).then_inc(aneg_done, 1)

            def step(name, b):
                if name == "xin":
                    me.start(b)
                elif name == "conv":
                    dve.wait_ge(S["xin_done"], b + 1)
                    dve.wait_ge(S["cv0_done"], b + 1)
                    for s in range(1, KC):
                        if s > 1:
                            me.wait()
                        for k in range(KD):
                            ins = dve.scalar_tensor_tensor(cv[:, k, s:], bb[:, k, 0:L - s],
                                                           cw[:, k, KC - 1 - s:KC - s], cv[:, k, s:],
                                                           ALU.mult, ALU.add)
                            if s < KC - 1:
                                me.did(ins)
                    ins.then_inc(S["conv_done"], 1)
                elif name == "u":
                    dve.wait_ge(S["econv_done"], b + 1)
                    me.then(dve.tensor_scalar(e1[:], e1[:], 1.0, None, ALU.add))
                    me.then(dve.reciprocal(rec[:], e1[:]))
                    dve.tensor_tensor(u[:], cv[:], rec[:], ALU.mult).then_inc(S["u_done"], 1)
                elif name == "split":
                    dve.wait_ge(S["bc0_done"], b + 1)
                    me.then(dve.tensor_tensor(bcr, misc[0:96, 0, :], bcs[:], ALU.subtract))
                    me.then(dve.tensor_copy(bcm, bcr))
                    dve.tensor_copy(bcs[32:64, :], bcm[32:64, :])
                    dve.tensor_tensor(bcs[64:96, :], bcr[64:96, :], bcm[64:96, :],
                                      ALU.subtract).then_inc(S["bcs_done"], 1)
                elif name == "stats":
                    dve.wait_ge(ld_xr, b * 16 + 16)
                    for k in range(KD):
                        me.did(dve.bn_stats(st6[:, k, :], xr[:, k, :]))
                    me.wait()
                    dve.memset(sink[:], 0.0)
                    for k in range(KD):
                        ins = dve.bn_aggr(mv[:, k, :], st6[:, k, :])
                    ins.then_inc(S["aggr_done"], 1)
                    dve.wait_ge(S["rs1_done"], b + 1)
                    dve.scalar_tensor_tensor(nb1[:], mv[:, :, 0], -1.0, rs1[:], ALU.mult,
                                             ALU.mult).then_inc(S["nb1_done"], 1)
                elif name == "delta":
                    dve.wait_ge(S["sp_done"], b + 1)
                    me.then(dve.tensor_tensor(delta[:], v[:], sp[:], ALU.add))
                    dve.tensor_tensor(du[:], delta[:], u[:], ALU.mult).then_inc(S["delta_done"], 1)
                elif name == "zgate":
                    dve.wait_ge(S["ez_done"], b + 1)
                    me.then(dve.tensor_scalar(e1[:], e1[:], 1.0, None, ALU.add))
                    me.then(dve.reciprocal(rec[:], e1[:]))
                    me.did(dve.tensor_tensor(sz[:], zz[:], rec[:], ALU.mult))
                elif type(name) is tuple:
                    c = name[1]
                    g = b * NC + c
                    if c:
                        dve.wait_ge(S["prod_done"], g)
                    else:
                        dve.wait_ge(S["delta_done"], b + 1)
                    dve.wait_ge(S["b_ready"], g + 1)
                    for k in range(KD):
                        ins = dve.tensor_tensor(bu[:, k, :].rearrange("p (j l) -> p j l", j=2), bb[:],
                                                du[:, k:k + 1, :].broadcast_to([P, 2, L]), ALU.mult)
                    ins.then_inc(S["bu_done"], 1)
                    dve.wait_ge(S["bu_done"], g + 1)
                    for k in range(KD):
                        dve.wait_ge(S["da_ready"], g * KD + k + 1)
                        for j in range(2):
                            one = slice(j * L, (j + 1) * L)
                            ins = dve.tensor_tensor_scan(bu[:, k, one], dA[:, k, one], bu[:, k, one], 0.0, ALU.mult,
                                                         ALU.add)
                        ins.then_inc(S["scan_done"], 1)
                    dve.wait_ge(S["c_ready"], g + 1)
                    for k in range(KD):
                        dve.wait_ge(S["scan_done"], g * KD + k + 1)
                        if first(name, b):
                            if c and k == 0:
                                dve.wait_ge(S["y_added"], c)
                        elif c > 1:
                            dve.wait_ge(S["y_folded"], ((b - 1) * NC + c - 2) * KD + k + 1)
                        dst = ya if c == 0 and not first(name, b) else pr
                        ins = dve.tensor_tensor(dst[:, k, :], bu[:, k, :], cc[:].rearrange("p a b -> p (a b)"), ALU.mult)
                    ins.then_inc(S["prod_done"], 1)
                elif name == "x1":
                    if first(name, b):
                        dve.wait_ge(S["y_added"], NC)
                    else:
                        dve.wait_ge(S["y_folded"], b * NC * KD)
                        dve.wait_ge(S["stored"], b * 16)
                    dve.wait_ge(ld_xT, b * 16 + 16)
                    ysum = acc if first(name, b) else y
                    for k in range(KD):
                        me.did(dve.scalar_tensor_tensor(y[:, k, :], u[:, k, :], dd[:, k:k + 1], ysum[:, k, :], ALU.mult,
                                                        ALU.add))
                    me.wait()
                    me.then(dve.tensor_tensor(y, y, sz[:], ALU.mult))
                    dve.tensor_tensor(x1[:, b % 2], y, xT[:], ALU.add).then_inc(S["x1_done"], 1)
                elif name == "centre":
                    dve.wait_ge(S["mean_done"], b + 1)
                    dve.tensor_tensor(xc[:], x1[:, b % 2], misc[:, 0:1, :].broadcast_to([P, KD, L]),
                                      ALU.subtract).then_inc(S["xc_done"], 1)
                elif name == "norm":
                    dve.wait_ge(S["r2_done"], b + 1)
                    me.then(dve.scalar_tensor_tensor(n1, misc[:, 0, :], EPS, r2, ALU.add, ALU.mult))
                    me.then(dve.tensor_tensor(n2, n1, r2, ALU.mult))
                    me.then(dve.tensor_scalar(n1, n2, -0.5, 1.5, ALU.mult, ALU.add))
                    me.then(dve.tensor_tensor(n2, n1, r2, ALU.mult))
                    dve.tensor_tensor(xs[:], xc[:], n2.rearrange("p (o l) -> p o l", o=1).broadcast_to([P, KD, L]),
                                      ALU.mult).then_inc(S["xs_done"], 1)
                    dve.wait_ge(S["xh_done"], b + 1)
                    dve.tensor_tensor(xl[:, b % 2], xs[:], xh[:, b % 2].bitcast(F32), ALU.subtract).then_inc(S["xl_done"], 1)
                elif name == "gates":
                    own.start(b)
                    dve.wait_ge(S["logits_done"], b + 1)
                    own.then(dve.tensor_tensor(lg[:, :, 0:NR], misc[:, :, 0:NR],
                                              rb.rearrange("p (o n) -> p o n", o=1).broadcast_to([P, 2, NR]), ALU.add))
                    dve.memset(sink[:], 0.0)
                    for t in range(2):
                        own.did(dve.max(m8[:, t, :], lg[:, t, 0:NR]))
                    own.wait()
                    dve.tensor_scalar(nm[:], m8[:, :, 0], -1.0, None, ALU.mult).then_inc(S["nm_done"], 1)
                    own.then(dve.memset(m8[:, :, TOPK:8], LOWEST))
                    dve.memset(sink[:], 0.0)
                    for t in range(2):
                        own.did(dve.match_replace(rep[:, t, :], m8[:, t, :], lg[:, t, :], HUGE))
                    own.wait()
                    own.then(dve.tensor_tensor(mask[:], rep[:, :, 0:NR], lg[:, :, 0:NR], ALU.not_equal))
                    dve.wait_ge(S["ex_done"], b + 1)
                    own.then(dve.tensor_tensor(em[:], ex[:], mask[:], ALU.mult))
                    own.then(dve.tensor_reduce(sm[:], em[:], AX.X, ALU.add))
                    own.then(dve.reciprocal(rsm[:], sm[:]))
                    for t in range(2):
                        own.did(dve.tensor_scalar(g34[:, t, 0:NR], em[:, t, :], rsm[:, t:t + 1], None, ALU.mult))
                    own.wait()
                    own.then(dve.tensor_copy(g3[:, :, 0, :], g34[:, :, 0:NR]))
                    own.then(dve.tensor_tensor(gr[:], g34[:, :, 0:NR], g3[:, :, 0, :], ALU.subtract))
                    own.then(dve.tensor_copy(g3[:, :, 1, :], gr[:]))
                    dve.tensor_tensor(g3[:, :, 2, :], gr[:], g3[:, :, 1, :], ALU.subtract).then_inc(S["g3_done"], 1)

            def pair(b, p):
                dve.wait_ge(S["relu_done"], b * NP + p + 1)
                n = len(PAIRS[p])
                if PAIRS[p][0] >= NT_S:
                    ins = dve.tensor_tensor(hg[:, p % 2], r[:, p % 2], gb[p % 2][:], ALU.mult)
                else:
                    ins = dve.tensor_scalar(hg[:, p % 2, 0:n], r[:, p % 2, 0:n], 1.0 / NSH, None, ALU.mult)
                ins.then_inc(S["hg_done"], 1)

            def end(b):
                dve.wait_ge(S["acc_done"], b + 1)
                dve.tensor_tensor(x1[:, b % 2], acc[:], x1[:, b % 2], ALU.add).then_inc(S["ot_done"], 1)

            run(dve, pair, end, step)

        @block.gpsimd
        def _(pool):
            for i in range(NW):
                a, e = i * WCH, min(NT, (i + 1) * WCH)
                pool.wait_ge(w1h_done, i + 1)
                pool.tensor_tensor(w1l[:, a:e, :].rearrange("p t m -> p (t m)"), stage[:, i % 2, 0:(e - a) * KD * P],
                                   w1h[:, a:e, :].rearrange("p t m -> p (t m)").bitcast(F32),
                                   ALU.subtract).then_inc(w1l_done, 1)

            def step(name, b):
                if first(name, b):
                    return
                if type(name) is tuple:
                    c = name[1]
                    if c == 0:
                        return
                    pool.wait_ge(S["prod_done"], b * NC + c + 1)
                    for k in range(KD):
                        if c > 1:
                            pool.wait_ge(S["y_folded"], ((b - 1) * NC + c - 2) * KD + k + 1)
                        pool.tensor_tensor(ya[:, k, :], ya[:, k, :], pr[:, k, :], ALU.add).then_inc(S["y_folded"], 1)
                elif name == "x1":
                    for k in range(KD):
                        pool.wait_ge(S["y_folded"], ((b - 1) * NC + NC - 2) * KD + k + 1)
                        pool.tensor_tensor(y[:, k, :], ya[:, k, 0:L], ya[:, k, L:2 * L],
                                           ALU.add).then_inc(S["y_folded"], 1)

            run(pool, nothing, nothing, step)


def kernel(**inputs):
    import ml_dtypes
    import numpy as np
    import concourse.bacc as bacc
    from concourse.bass_utils import run_bass_kernel_spmd

    def get(n):
        return np.asarray(inputs[n])

    def halves(a):
        return a.reshape((KD, P) + a.shape[1:]).swapaxes(0, 1)

    x = get("x")
    xa = {k: get("L0_xattn_" + k) for k in ("in_proj_w", "conv_w", "conv_b", "x_proj_w", "dt_proj_w", "dt_proj_b",
                                            "A_log", "D")}
    ff = {k: get("L0_ffn_" + k) for k in ("sw1", "sb1", "sw2", "sb2", "rw1", "rb1", "rw2", "rb2", "router_w",
                                          "router_b")}
    f32 = x.dtype
    ns, off = NSH * HID, NT_S * P
    w1 = np.zeros((DX, NT * P), f32)
    w1[:, :ns] = ff["sw1"].transpose(1, 0, 2).reshape(DX, -1)
    w1[:, off:] = ff["rw1"].transpose(1, 0, 2).reshape(DX, -1)
    w2 = np.zeros((NT * P, DX), f32)
    w2[:ns] = ff["sw2"].reshape(-1, DX)
    w2[off:] = ff["rw2"].reshape(-1, DX)
    b1 = np.zeros((NT * P,), f32)
    b1[:ns] = ff["sb1"].reshape(-1)
    b1[off:] = ff["rb1"].reshape(-1)
    w1 = w1.reshape(KD, P, NT, P).transpose(1, 2, 0, 3).reshape(P, NT, KD * P)
    w2 = w2.reshape(NT, P, DX).transpose(1, 0, 2)
    xp = halves(xa["x_proj_w"].T)
    par = np.zeros((P, NPAR), f32)

    def put(name, a):
        par[:, PAR[name][0]:PAR[name][1]] = a.reshape(P, -1)

    put("win", xa["in_proj_w"].T)
    put("xbc", np.concatenate([xp[:, :, DR:]] * 3, axis=2))
    put("xdt", xp[:, :, :DR])
    put("cw", halves(xa["conv_w"]))
    put("cb", halves(xa["conv_b"]))
    put("dtb", halves(xa["dt_proj_b"]))
    put("alog", halves(xa["A_log"]))
    put("dd", halves(xa["D"]))
    put("rw", halves(ff["router_w"]))
    put("rb", np.broadcast_to(ff["router_b"], (P, NR)))
    put("b1", b1.reshape(NT, P).T)
    put("ident", np.eye(P, dtype=f32))
    small = np.zeros((NR + NSH, 2 * DX), f32)
    small[:DR, :DX] = xa["dt_proj_w"].T
    small[:NR, DX:] = ff["rb2"]
    small[NR:, DX:] = ff["sb2"]
    expert = np.arange(NR * HID) // HID
    selg = np.tile((expert[None, :] == np.arange(NR)[:, None]), (3, 1)).astype(ml_dtypes.bfloat16)
    selbc = np.tile(np.eye(2 * NS), (3, 1)).astype(ml_dtypes.bfloat16)
    arrays = {
        "in_xT": halves(x.transpose(2, 0, 1)),
        "in_xr": halves(x.transpose(1, 0, 2)),
        "in_ctx": get("ctx_1024").transpose(2, 0, 1),
        "in_par": par,
        "in_small": small,
        "in_w1": w1,
        "in_w2": w2,
        "in_selg": selg.reshape(3 * NR, NT_R, P),
        "in_selbc": selbc,
    }
    arrays = {k: np.ascontiguousarray(a) for k, a in arrays.items()}
    nc = bacc.Bacc("TRN2", target_bir_lowering=False, num_devices=1, dynamic_dma_scratch_size=1024)
    args = [nc.dram_tensor(k, a.shape, mybir.dt.from_np(a.dtype), kind="ExternalInput").ap() for k, a in arrays.items()]
    out = nc.dram_tensor("out_0", (P, KD, B, L), F32, kind="ExternalOutput").ap()
    xattn_ffn_kernel(nc, *args, out)
    r = run_bass_kernel_spmd(nc, [arrays], core_ids=[0])
    o = r.results[0]["out_0"]
    return np.ascontiguousarray(o.transpose(2, 3, 1, 0).reshape(B, L, DX))
```

```python
from contextlib import ExitStack

import concourse.bass as bass
from concourse import mybir

F32 = mybir.dt.float32
F32R = mybir.dt.float32r
BF16 = mybir.dt.bfloat16
ALU = mybir.AluOpType
ACT = mybir.ActivationFunctionType
AX = mybir.AxisListType

P = 128
B, L, DX = 4, 256, 256
DC_IN = 128
KD = DX // P
NS, DR, KC = 16, 8, 4
NR, NSH, HID, TOPK = 32, 2, 176, 6
NT_S = -(-NSH * HID // P)
NT_R = NR * HID // P
NT = NT_S + NT_R
PAIRS = [[0, 1], [2]] + [[t, t + 1] for t in range(NT_S, NT, 2)]
NP = len(PAIRS)
NPR = NT_R // 2
NC = NS // 2
EPS = 1e-5
LOWEST = -3.0e38
HUGE = 3.0e38
WCH = 4
NW = -(-NT // WCH)

PAR = {}
_at = 0
for _name, _n in (("win", DX), ("cw", KD * KC), ("cb", KD), ("xbc", KD * 3 * 2 * NS), ("xdt", KD * DR), ("dtb", KD),
                  ("alog", KD * NS), ("dd", KD), ("rw", KD * NR), ("rb", NR), ("b1", NT), ("ident", P)):
    PAR[_name] = (_at, _at + _n)
    _at += _n
NPAR = _at
NPAR_EARLY = PAR["cb"][1]

CHUNKS = [(("chunk", c), at) for c, at in enumerate([6, 8, 9, 10, 11, 13, 14, 15])]
FRONT = [("xin", 0), ("cv0", 0), ("stats", 0), ("taps", 0), ("rs1", 1), ("econv", 1), ("nb1", 1), ("uclip", 1),
         ("usig", 3), ("u", 3), ("xdt", 4), ("dtl", 4), ("zsig", 3), ("zmul", 5), ("dt", 5), ("xbc", 5), ("split", 5), ("sp", 5),
         ("delta", 5)]
BACK = [("x1", 17), ("mean", 19), ("centre", 19), ("var", 20), ("r2", 20), ("norm", 21), ("xh", 23), ("logits", 23),
        ("xl", 23), ("top", 23), ("ex", 23), ("gates", 23)]
STEPS = FRONT + CHUNKS + BACK
PROLOGUE = ["xin", "stats", "rs1", "cv0", "nb1", "zsig", "taps", "econv", "uclip", "usig", "u", "xdt", "dtl", "xbc", "dt",
            "zmul", "split", "sp", "delta"] + [n for n, _ in CHUNKS + BACK]
assert sorted(map(str, PROLOGUE)) == sorted(str(n) for n, _ in STEPS)
TURN_AT = 1
SKEW = 3
RING = 6
SPLIT = [0, 2, 3, 11, 12, 14, 19, 20, 21]
BIG = 2.0 ** 63


def xattn_ffn_kernel(nc: bass.Bass, xT_d, xr_d, ctx_d, par_d, small_d, w1_d, w2_d, selg_d, selbc_d, out_d):
    ctx = ExitStack()
    with ctx:
        def sb(name, shape, dt=F32):
            return ctx.enter_context(nc.sbuf_tensor(name, shape, dt))

        def ps(name, shape, dt=F32):
            return ctx.enter_context(nc.psum_tensor(name, shape, dt))

        def sem(name):
            return ctx.enter_context(nc.semaphore(name))

        xr = sb("xr", [P, B, KD, DX])
        ctxT = sb("ctxT", [P, B, L])
        par = sb("par", [P, NPAR])
        small = sb("small", [NR + NSH, 2 * DX])
        w1h = sb("w1h", [P, NT, KD * P], F32R)
        w1l = sb("w1l", [P, NT, KD * P], F32R)
        w2 = sb("w2", [P, RING, 2, DX])
        w2l = sb("w2l", [P, 4, 2, DX], F32R)
        w2h = sb("w2h", [P, 4, 2, DX], F32R)
        selg = sb("selg", [3 * NR, NT_R, P], BF16)
        selbc = sb("selbc", [3 * 2 * NS, 2 * NS], BF16)

        def pv(name):
            return par[:, PAR[name][0]:PAR[name][1]]

        win, cb, dtb, dd, rb, b1, ident = (pv(n) for n in ("win", "cb", "dtb", "dd", "rb", "b1", "ident"))
        xbc = pv("xbc").rearrange("p (k m) -> p k m", k=KD)
        xdt = pv("xdt").rearrange("p (k m) -> p k m", k=KD)
        cw = pv("cw").rearrange("p (k m) -> p k m", k=KD)
        rw = pv("rw").rearrange("p (k m) -> p k m", k=KD)
        dtw = small[0:DR, 0:DX]
        b2x = small[:, DX:2 * DX]

        identb = sb("identb", [P, P], BF16)
        meanw = sb("meanw", [P, P])
        aneg = sb("aneg", [P, KD * NS])
        epsc = sb("epsc", [P, 1])
        st6 = sb("st6", [P, KD, 6])
        mv = sb("mv", [P, KD, 2])
        rs1 = sb("rs1", [P, KD])
        nb1 = sb("nb1", [P, KD])
        cv = sb("cv", [P, KD, L])
        e1 = sb("e1", [P, KD, L])
        rec = sb("rec", [P, KD, L])
        u = sb("u", [P, KD, L])
        bcs = sb("bcs", [96, L], BF16)
        delta = sb("delta", [P, KD, L])
        du = sb("du", [P, KD, L])
        sz = sb("sz", [P, KD, L])
        dA = sb("dA", [P, KD, 2 * L])
        bu = sb("bu", [P, KD, 2 * L])
        pr = sb("pr", [P, KD, 2 * L])
        ya = sb("ya", [P, KD, 2 * L])
        x1 = sb("x1", [P, 2, KD, L])
        bcr, bcm, dtl = dA[0:96, 0, 0:L], dA[0:96, 1, 0:L // 2].bitcast(BF16), rec[0:DR, 0, :]
        v, sp = rec, e1
        y = pr[:, :, 0:L]
        xc, sq, xs = e1, y, delta
        cs = cv[:].rearrange("p k l -> p (k l)")
        ez = du
        r2, n1, n2 = cv[:, 0, :], cv[:, 1, :], rec[:, 0, :]
        xh = sb("xh", [P, 2, KD, L], F32R)
        xl = sb("xl", [P, 2, KD, L], F32R)
        lg = sb("lg", [P, 2, NR + 2])
        m8 = sb("m8", [P, 2, 8])
        nm = sb("nm", [P, 2])
        sink = sb("sink", [P, 1])
        rep = sb("rep", [P, 2, NR + 2])
        ex = sb("ex", [P, 2, NR])
        mask = sb("mask", [P, 2, NR])
        em = sb("em", [P, 2, NR])
        sm = sb("sm", [P, 2])
        rsm = sb("rsm", [P, 2])
        g34 = sb("g34", [P, 2, NR + NSH])
        gr = sb("gr", [P, 2, NR])
        g3 = sb("g3", [P, 2, 3, NR], BF16)
        gst = sb("gst", [3 * NR, L], BF16)
        gT = sb("gT", [NR + NSH, L])
        stage = sb("stage", [P, 2, WCH * KD * P])
        hg = stage[:].rearrange("p h (a b l) -> p (h a) b l", a=2, b=2)
        hh = sb("hh", [P, 4, 2, L], F32R)
        hl = sb("hl", [P, 4, 2, L], F32R)

        z = [ps(f"z{i}", [P, 2, L]) for i in range(2)]
        gb = [ps(f"gb{i}", [P, 2, L]) for i in range(2)]
        acc = ps("acc", [P, KD, L])
        bb = ps("bb", [P, 2, L])
        cc = ps("cc", [P, 2, L])
        misc = ps("misc", [P, 2, L])
        miscb = misc[:].rearrange("p a b -> p (a b)").bitcast(BF16)

        ld_early = sem("ld_early")
        ld_ctx, ld_par, ld_xr, ld_xT, ld_sel, ld_selg = (sem(n) for n in
                                                         ("ld_ctx", "ld_par", "ld_xr", "ld_xT", "ld_sel", "ld_selg"))
        ld_w1 = [sem(f"ld_w1_{i}") for i in range(2)]
        ld_w2 = [sem(f"ld_w2_{i}") for i in range(RING)]
        w1h_done, w1l_done = sem("w1h_done"), sem("w1l_done")
        dve_step, dve_router_step, act_step = sem("dve_step"), sem("dve_router_step"), sem("act_step")
        aexp_done, aneg_done, const_done = sem("aexp_done"), sem("aneg_done"), sem("const_done")
        names = ["xin_done", "conv_done", "econv_done", "u_done", "dtlo_done", "xbc_done", "dtl_done", "bcs_done", "dt_done",
                 "v_done", "sp_done", "delta_done", "zz_done", "ez_done", "b_ready", "c_ready", "bu_done", "da_ready",
                 "scan_done", "prod_done", "y_folded", "x1_done", "xs_done", "mean_done", "sq_done", "var_done", "r2_done",
                 "xh_done", "xl_done", "logits_done", "nm_done", "ex_done", "g3_done", "turned", "gates_done",
                 "z_ready", "relu_done", "hg_done", "acc_done", "ot_done", "stored", "aggr_done", "rs1_done", "nb1_done",
                 "cv0_done", "y_added", "uclip_done", "usig_done", "gb_ready", "hh_done", "hl_done", "w2h_done", "w2l_done",
                 "l2_done", "c_copied", "pool_prod_done"]
        S = {n: sem(n) for n in names}

        block = ctx.enter_context(nc.Block())

        def wait_w2(eng, b, p):
            eng.wait_ge(ld_w2[p % RING], b * (16 * NP // RING) + 16 * (p // RING + 1))

        class Steps:

            def __init__(self, eng, s, per):
                self.eng, self.s, self.n, self.per, self.base = eng, s, per, per, 0

            def start(self, b):
                assert self.n == self.per, self.n
                self.n, self.base = 0, b * self.per

            def did(self, ins):
                ins.then_inc(self.s, 1)
                self.n += 1

            def wait(self):
                self.eng.wait_ge(self.s, self.base + self.n)

            def then(self, ins):
                self.did(ins)
                self.wait()

        def run(eng, ffn_pair, ffn_end, step):
            for name in PROLOGUE:
                step(name, 0)
            with eng.Fori(0, B - 1) as i:
                for p in range(NP):
                    ffn_pair(i, p, True)
                ffn_end(i)
            for p in range(NP):
                ffn_pair(B - 1, p, False)
            ffn_end(B - 1)

        def nothing(*_):
            pass

        def beside(p, step, b):
            for name, at in STEPS:
                if at == p:
                    step(name, b)

        def split(b, p):
            return type(b) is int or p in SPLIT

        def nth_split(b, p):
            return b * len(SPLIT) + sum(split(b, q) for q in range(p + 1))

        def products(b, c):
            return (pr, ya)[c % 2] if type(b) is int else (pr if c else ya)

        def first(name, b):
            return type(b) is int and b == 0

        @block.sync
        def _(eng):
            eng.dma_start(par[:, 0:NPAR_EARLY], par_d[:, 0:NPAR_EARLY]).then_inc(ld_early, 16)
            eng.dma_start(ctxT[:, 0], ctx_d[:, 0]).then_inc(ld_early, 16)
            eng.dma_start(xr[:, 0], xr_d[:, 0]).then_inc(ld_xr, 16)
            eng.dma_start(par[:, NPAR_EARLY:], par_d[:, NPAR_EARLY:]).then_inc(ld_par, 16)
            eng.dma_start(small[:], small_d).then_inc(ld_par, 16)
            eng.dma_start(selbc[:], selbc_d).then_inc(ld_sel, 16)
            eng.dma_start(x1[:, 0], xT_d[:, :, 0, :]).then_inc(ld_xT, 16)
            for i in range(NW):
                a, e = i * WCH, min(NT, (i + 1) * WCH)
                if i >= 2:
                    eng.wait_ge(w1l_done, i - 1)
                eng.dma_start(stage[:, i % 2, 0:(e - a) * KD * P].rearrange("p (t m) -> p t m", m=KD * P),
                              w1_d[:, a:e, :]).then_inc(ld_w1[i % 2], 16)
            eng.dma_start(selg[:], selg_d).then_inc(ld_selg, 16)

            def load_w2(p):
                t, n = PAIRS[p][0], len(PAIRS[p])
                eng.dma_start(w2[:, p % RING, 0:n, :], w2_d[:, t:t + n, :]).then_inc(ld_w2[p % RING], 16)

            for p in range(RING):
                load_w2(p)
            eng.dma_start(xr[:, 1:], xr_d[:, 1:]).then_inc(ld_xr, 16)
            eng.dma_start(ctxT[:, 1:], ctx_d[:, 1:]).then_inc(ld_ctx, 16)

            def store(b):
                eng.wait_ge(S["ot_done"], b + 2)
                eng.dma_start(out_d[:, :, b, :], x1[:, b % 2]).then_inc(S["stored"], 16)

            with eng.Fori(0, B - 1) as i:
                eng.wait_ge(S["stored"], 16 * i + 16)
                eng.dma_start(x1[:, (i + 1) % 2], xT_d[:, :, i + 1, :]).then_inc(ld_xT, 16)
                for p in range(NP):
                    eng.wait_ge(S["l2_done"], i * NP + p + 1)
                    load_w2((p + RING) % NP)
                store(i)
            for p in range(NP - RING):
                eng.wait_ge(S["l2_done"], (B - 1) * NP + p + 1)
                load_w2(p + RING)
            store(B - 1)
            eng.wait_ge(S["stored"], 16 * (B + 1))

        @block.tensor
        def _(pe):
            def sum_states(c):
                for k in range(KD):
                    for j in range(2):
                        if j == 0:
                            pe.wait_ge(S[("prod_done", "pool_prod_done")[k]], c + 1)
                        mm = pe.matmul(acc[:, k, :], ident, (pr, ya)[c % 2][:, k, j * L:(j + 1) * L],
                                       start=c + k + j == 0, stop=c == NC - 1 and j == 1, skip_group_check=True)
                mm.then_inc(S["y_added"], 1)

            def b_step(name, b):
                if type(name) is tuple:
                    c = name[1]
                    if c == 0:
                        if type(b) is int:
                            pe.wait_ge(ld_sel, 16)
                        pe.wait_ge(S["bcs_done"], b + 1)
                        pe.wait_ge(S["sp_done"], b + 1)
                    else:
                        pe.wait_ge(S["bu_done"], b * NC + c)
                    for j in range(2):
                        mm = pe.matmul(bb[:, j, :], selbc[:, 2 * c + j:2 * c + j + 1].broadcast_to([96, P]), bcs[:],
                                       start=True, stop=True)
                    mm.then_inc(S["b_ready"], 1)

            def step(name, b):
                if name == "xin":
                    if first(name, b):
                        pe.wait_ge(ld_early, 32)
                    else:
                        pe.wait_ge(ld_ctx, 16)
                    for k in range(KD):
                        mm = pe.matmul(bb[:, k, :], win[:, k * P:(k + 1) * P], ctxT[:, b, :], start=True, stop=True)
                    mm.then_inc(S["xin_done"], 1)
                elif name == "xdt":
                    if first(name, b):
                        pe.wait_ge(ld_par, 32)
                    pe.wait_ge(S["u_done"], b + 1)
                    for k in range(KD):
                        mm = pe.matmul(cc[0:DR, 0, :], xdt[:, k, :], u[:, k, :], start=k == 0, stop=k == KD - 1)
                    mm.then_inc(S["dtlo_done"], 1)
                elif name == "xbc":
                    for k in range(KD):
                        mm = pe.matmul(misc[0:96, 0, :], xbc[:, k, :], u[:, k, :], start=k == 0, stop=k == KD - 1)
                    mm.then_inc(S["xbc_done"], 1)
                elif name == "dt":
                    pe.wait_ge(S["dtl_done"], b + 1)
                    for k in range(KD):
                        mm = pe.matmul(bb[:, k, :], dtw[:, k * P:(k + 1) * P], dtl, start=True, stop=True)
                    mm.then_inc(S["dt_done"], 1)
                elif type(name) is tuple:
                    c = name[1]
                    if c:
                        pe.wait_ge(S["c_copied"], b * NC + c)
                    for j in range(2):
                        n = NS + 2 * c + j
                        mm = pe.matmul(cc[:, j, :], selbc[:, n:n + 1].broadcast_to([96, P]), bcs[:],
                                       start=True, stop=True)
                    mm.then_inc(S["c_ready"], 1)
                    if first(name, b):
                        if c:
                            sum_states(c - 1)
                        if c == NC - 1:
                            sum_states(c)
                elif name == "mean":
                    if type(b) is int:
                        pe.wait_ge(const_done, 3)
                    pe.wait_ge(S["x1_done"], b + 1)
                    for k in range(KD):
                        mm = pe.matmul(misc[:, 0, :], meanw[:], x1[:, b % 2, k, :], start=k == 0, stop=k == KD - 1)
                    mm.then_inc(S["mean_done"], 1)
                elif name == "var":
                    pe.wait_ge(S["sq_done"], b + 1)
                    for k in range(KD):
                        mm = pe.matmul(misc[:, 0, :], meanw[:], sq[:, k, :], start=k == 0, stop=k == KD - 1)
                    mm.then_inc(S["var_done"], 1)
                elif name == "logits":
                    pe.wait_ge(S["xs_done"], b + 1)
                    for t in range(2):
                        for k in range(KD):
                            mm = pe.matmul(misc[:, t, 0:NR], xs[:, k, t * P:(t + 1) * P], rw[:, k, :],
                                           start=k == 0, stop=k == KD - 1)
                    mm.then_inc(S["logits_done"], 1)

            def turn(b):
                pe.wait_ge(S["g3_done"], b + 1)
                for t in range(2):
                    pe.transpose(miscb[0:3 * NR, t * P:(t + 1) * P], g3[:, t].rearrange("p a b -> p (a b)"), identb[:])
                for t in range(2):
                    mm = pe.transpose(misc[0:NR + NSH, 1, t * P:(t + 1) * P], g34[:, t, :], ident)
                mm.then_inc(S["turned"], 1)

            def second_layer(b, p):
                if split(b, p):
                    pe.wait_ge(S["hl_done"], nth_split(b, p))
                    pe.wait_ge(S["w2l_done"], nth_split(b, p))
                else:
                    pe.wait_ge(S["hg_done"], b * NP + p + 1)
                    wait_w2(pe, b, p)
                if p == 0:
                    pe.wait_ge(S["ot_done"], b + 1)
                for i, t in enumerate(PAIRS[p]):
                    for k in range(KD):
                        one = slice(k * P, (k + 1) * P)
                        parts = [(w2[:, p % RING, i, one], hg[:, p % 4, i, :])]
                        if split(b, p):
                            lo, hi = w2l[:, p % 4, i, one], w2h[:, p % 4, i, one]
                            parts = [(lo, hh[:, p % 4, i, :]), (hi, hl[:, p % 4, i, :]), (hi, hh[:, p % 4, i, :])]
                        for n, (weights, h) in enumerate(parts):
                            mm = pe.matmul(acc[:, k, :], weights, h, start=t + k + n == 0, stop=False,
                                           skip_group_check=True)
                mm.then_inc(S["l2_done"], 1)
                if p == NP - 1:
                    for k in range(KD):
                        mm = pe.matmul(acc[:, k, :], b2x[:, k * P:(k + 1) * P], gT[:], start=False, stop=True,
                                       skip_group_check=True)
                    mm.then_inc(S["acc_done"], 1)

            def pair(b, p, more):
                if p == 0:
                    pe.wait_ge(S["xl_done"], b + 1)
                if p >= 2:
                    pe.wait_ge(S["hg_done"], b * NP + p - 1)
                for i, t in enumerate(PAIRS[p]):
                    if t % WCH == 0:
                        pe.wait_ge(w1l_done, t // WCH + 1)
                    for k in range(KD):
                        one = slice(k * P, (k + 1) * P)
                        xh_, xl_ = xh[:, b % 2, k, :], xl[:, b % 2, k, :]
                        pe.matmul(z[p % 2][:, i, :], w1l[:, t, one], xh_, start=k == 0, stop=False)
                        pe.matmul(z[p % 2][:, i, :], w1h[:, t, one], xl_, start=False, stop=False)
                        mm = pe.matmul(z[p % 2][:, i, :], w1h[:, t, one], xh_, start=False, stop=k == KD - 1)
                mm.then_inc(S["z_ready"], 1)
                if PAIRS[p][0] >= NT_S:
                    if PAIRS[p][0] == NT_S:
                        pe.wait_ge(ld_selg, 16)
                        pe.wait_ge(S["gates_done"], b + 1)
                    for i, t in enumerate(PAIRS[p]):
                        mm = pe.matmul(gb[p % 2][:, i, :], selg[:, t - NT_S, :], gst[:], start=True, stop=True)
                    mm.then_inc(S["gb_ready"], 1)
                if p == TURN_AT:
                    turn(b)
                if more:
                    beside(p, b_step, b + 1)
                if p >= SKEW:
                    second_layer(b, p - SKEW)
                if more:
                    beside(p, step, b + 1)

            def end(b):
                for p in range(NP - SKEW, NP):
                    second_layer(b, p)

            def b_then_step(name, b):
                b_step(name, b)
                step(name, b)

            run(pe, pair, end, b_then_step)

        @block.scalar
        def _(act):
            me = Steps(act, act_step, 7)
            act.preload_act_table_set("natural_log_exp_and_others")
            todo = list(range(NW))

            def split_w1(n):
                for i in todo[:n]:
                    a, e = i * WCH, min(NT, (i + 1) * WCH)
                    act.wait_ge(ld_w1[i % 2], 16 * (i // 2 + 1))
                    act.activation(w1h[:, a:e, :].rearrange("p t m -> p (t m)"), stage[:, i % 2, 0:(e - a) * KD * P],
                                   ACT.Copy).then_inc(w1h_done, 1)
                del todo[:n]

            def step(name, b):
                if name == "xin":
                    me.start(b)
                elif name == "rs1":
                    act.wait_ge(S["aggr_done"], b + 1)
                    me.then(act.activation(rs1[:], mv[:, :, 1], ACT.Ln, bias=epsc[:]))
                    act.activation(rs1[:], rs1[:], ACT.Exp, scale=-0.5).then_inc(S["rs1_done"], 1)
                elif name == "cv0":
                    if first(name, b):
                        act.wait_ge(ld_early, 32)
                    act.wait_ge(S["xin_done"], b + 1)
                    for k in range(KD):
                        ins = act.activation(cv[:, k, :], bb[:, k, :], ACT.Identity, scale=cw[:, k, KC - 1:KC],
                                             bias=cb[:, k:k + 1])
                    ins.then_inc(S["cv0_done"], 1)
                elif name == "econv":
                    act.wait_ge(S["conv_done"], b + 1)
                    act.activation(e1[:], cv[:], ACT.Exp, scale=-1.0).then_inc(S["econv_done"], 1)
                elif name == "usig":
                    if first(name, b):
                        act.wait_ge(ld_par, 32)
                        act.activation(aneg[:], pv("alog"), ACT.Exp).then_inc(aexp_done, 1)
                    act.wait_ge(S["uclip_done"], b + 1)
                    me.then(act.activation(e1[:], e1[:], ACT.Ln))
                    act.activation(e1[:], e1[:], ACT.Exp, scale=-1.0).then_inc(S["usig_done"], 1)
                    if first(name, b):
                        split_w1(1)
                elif name == "zsig":
                    act.wait_ge(S["nb1_done"], b + 1)
                    for k in range(KD):
                        ins = act.activation(sz[:, k, :], xr[:, b, k, :], ACT.Identity, scale=rs1[:, k:k + 1],
                                             bias=nb1[:, k:k + 1])
                    ins.then_inc(S["zz_done"], 1)
                    act.wait_ge(S["zz_done"], b + 1)
                    me.then(act.activation(ez[:], sz[:], ACT.Exp, scale=-1.0))
                    me.then(act.activation(ez[:], ez[:], ACT.Ln, bias=1.0))
                    act.activation(ez[:], ez[:], ACT.Exp, scale=-1.0).then_inc(S["ez_done"], 1)
                elif name == "dtl":
                    act.wait_ge(S["dtlo_done"], b + 1)
                    act.activation(dtl, cc[0:DR, 0, :], ACT.Copy).then_inc(S["dtl_done"], 1)
                    if first(name, b):
                        split_w1(1)
                elif name == "sp":
                    act.wait_ge(S["dt_done"], b + 1)
                    for k in range(KD):
                        ins = act.activation(sp[:, k, :], bb[:, k, :], ACT.Abs, bias=dtb[:, k:k + 1])
                    me.then(ins)
                    me.did(act.activation(sp[:], sp[:], ACT.Exp, scale=-1.0))
                    for k in range(KD):
                        act.activation(v[:, k, :], bb[:, k, :], ACT.Relu, bias=dtb[:, k:k + 1])
                    me.wait()
                    act.activation(sp[:], sp[:], ACT.Ln, bias=1.0).then_inc(S["sp_done"], 1)
                    if first(name, b):
                        split_w1(1)
                elif type(name) is tuple:
                    c = name[1]
                    if c == 0:
                        act.wait_ge(S["delta_done"], b + 1)
                        if first(name, b):
                            act.wait_ge(aneg_done, 1)
                    for k in range(KD):
                        if c:
                            act.wait_ge(S["scan_done"], (b * NC + c - 1) * KD + k + 1)
                        for j in range(2):
                            n = k * NS + 2 * c + j
                            ins = act.activation(dA[:, k, j * L:(j + 1) * L], delta[:, k, :], ACT.Exp,
                                                 scale=aneg[:, n:n + 1])
                        ins.then_inc(S["da_ready"], 1)
                    act.wait_ge(S["c_ready"], b * NC + c + 1)
                    if c:
                        act.wait_ge(S["prod_done"], b * NC + c)
                        act.wait_ge(S["pool_prod_done"], b * NC + c)
                    act.activation(cs, cc[:].rearrange("p a b -> p (a b)"), ACT.Copy).then_inc(S["c_copied"], 1)
                    if first(name, b):
                        split_w1(1)
                elif name == "x1":
                    if first(name, b):
                        split_w1(len(todo))
                elif name == "r2":
                    act.wait_ge(S["var_done"], b + 1)
                    me.then(act.activation(r2, misc[:, 0, :], ACT.Ln, bias=epsc[:]))
                    act.activation(r2, r2, ACT.Exp, scale=-0.5).then_inc(S["r2_done"], 1)
                elif name == "xh":
                    act.wait_ge(S["xs_done"], b + 1)
                    act.activation(xh[:, b % 2], xs[:], ACT.Copy).then_inc(S["xh_done"], 1)
                elif name == "ex":
                    act.wait_ge(S["nm_done"], b + 1)
                    for t in range(2):
                        ins = act.activation(ex[:, t, :], lg[:, t, 0:NR], ACT.Exp, bias=nm[:, t:t + 1])
                    ins.then_inc(S["ex_done"], 1)

            def pair(b, p, more):
                if first("pair", b) or p == 0:
                    act.wait_ge(w1l_done, NW)
                act.wait_ge(S["z_ready"], b * NP + p + 1)
                for i, t in enumerate(PAIRS[p]):
                    ins = act.activation(hg[:, p % 4, i, :], z[p % 2][:, i, :], ACT.Relu, bias=b1[:, t:t + 1])
                ins.then_inc(S["relu_done"], 1)
                if p and split(b, p - 1):
                    upper_h(b, p - 1)
                if split(b, p):
                    n = len(PAIRS[p])
                    wait_w2(act, b, p)
                    act.activation(w2h[:, p % 4, 0:n, :], w2[:, p % RING, 0:n, :], ACT.Copy).then_inc(S["w2h_done"], 1)
                if p == TURN_AT:
                    act.wait_ge(S["turned"], b + 1)
                    act.activation(gst[:], miscb[0:3 * NR, 0:L], ACT.Copy)
                    act.activation(gT[:], misc[0:NR + NSH, 1, :], ACT.Copy).then_inc(S["gates_done"], 1)
                if more:
                    beside(p, step, b + 1)

            def upper_h(b, p):
                n = len(PAIRS[p])
                act.wait_ge(S["hg_done"], b * NP + p + 1)
                act.activation(hh[:, p % 4, 0:n], hg[:, p % 4, 0:n], ACT.Copy).then_inc(S["hh_done"], 1)

            def end(b):
                if split(b, NP - 1):
                    upper_h(b, NP - 1)

            run(act, pair, end, step)

        @block.vector
        def _(dve):
            me, own = Steps(dve, dve_step, 19), Steps(dve, dve_router_step, 15)
            dve.memset(epsc[:], EPS).then_inc(const_done, 1)
            dve.memset(meanw[:], 1.0 / DX).then_inc(const_done, 1)
            dve.memset(lg[:], LOWEST).then_inc(S["ot_done"], 1)
            dve.memset(g34[:], 1.0 / NSH).then_inc(S["stored"], 16)

            def step(name, b):
                if name == "xin":
                    me.start(b)
                elif name == "taps":
                    if first(name, b):
                        dve.wait_ge(ld_early, 32)
                    dve.wait_ge(S["xin_done"], b + 1)
                    dve.wait_ge(S["cv0_done"], b + 1)
                    for s in range(1, KC):
                        if s > 1:
                            me.wait()
                        for k in range(KD):
                            ins = dve.scalar_tensor_tensor(cv[:, k, s:], bb[:, k, 0:L - s],
                                                           cw[:, k, KC - 1 - s:KC - s], cv[:, k, s:],
                                                           ALU.mult, ALU.add)
                            if s < KC - 1:
                                me.did(ins)
                    ins.then_inc(S["conv_done"], 1)
                elif name == "uclip":
                    dve.wait_ge(S["econv_done"], b + 1)
                    dve.tensor_scalar(e1[:], e1[:], BIG, 1.0, ALU.min, ALU.add).then_inc(S["uclip_done"], 1)
                elif name == "u":
                    if first(name, b):
                        dve.wait_ge(ld_par, 32)
                        dve.tensor_copy(identb[:], ident).then_inc(const_done, 1)
                        dve.wait_ge(aexp_done, 1)
                        dve.tensor_scalar(aneg[:], aneg[:], -1.0, None, ALU.mult).then_inc(aneg_done, 1)
                    dve.wait_ge(S["usig_done"], b + 1)
                    dve.tensor_tensor(u[:], cv[:], e1[:], ALU.mult).then_inc(S["u_done"], 1)
                elif name == "split":
                    dve.wait_ge(S["xbc_done"], b + 1)
                    me.then(dve.tensor_copy(bcs[:], misc[0:96, 0, :]))
                    me.then(dve.tensor_tensor(bcr, misc[0:96, 0, :], bcs[:], ALU.subtract))
                    me.then(dve.tensor_copy(bcm, bcr))
                    dve.tensor_copy(bcs[32:64, :], bcm[32:64, :])
                    dve.tensor_tensor(bcs[64:96, :], bcr[64:96, :], bcm[64:96, :],
                                      ALU.subtract).then_inc(S["bcs_done"], 1)
                elif name == "stats":
                    dve.wait_ge(ld_xr, 16 if first(name, b) else 32)
                    for k in range(KD):
                        me.did(dve.bn_stats(st6[:, k, :], xr[:, b, k, :]))
                    me.wait()
                    dve.memset(sink[:], 0.0)
                    for k in range(KD):
                        ins = dve.bn_aggr(mv[:, k, :], st6[:, k, :])
                    ins.then_inc(S["aggr_done"], 1)
                elif name == "nb1":
                    dve.wait_ge(S["rs1_done"], b + 1)
                    dve.scalar_tensor_tensor(nb1[:], mv[:, :, 0], -1.0, rs1[:], ALU.mult,
                                             ALU.mult).then_inc(S["nb1_done"], 1)
                elif name == "delta":
                    dve.wait_ge(S["sp_done"], b + 1)
                    me.then(dve.tensor_tensor(delta[:], v[:], sp[:], ALU.add))
                    dve.tensor_tensor(du[:], delta[:], u[:], ALU.mult).then_inc(S["delta_done"], 1)
                elif name == "zmul":
                    dve.wait_ge(S["ez_done"], b + 1)
                    me.did(dve.tensor_tensor(sz[:], sz[:], ez[:], ALU.mult))
                elif type(name) is tuple:
                    c = name[1]
                    g = b * NC + c
                    if c == 0:
                        dve.wait_ge(S["delta_done"], b + 1)
                    dve.wait_ge(S["b_ready"], g + 1)
                    for k in range(KD):
                        if c:
                            dve.wait_ge(S[("prod_done", "pool_prod_done")[k]], g)
                        ins = dve.tensor_tensor(bu[:, k, :].rearrange("p (j l) -> p j l", j=2), bb[:],
                                                du[:, k:k + 1, :].broadcast_to([P, 2, L]), ALU.mult)
                    ins.then_inc(S["bu_done"], 1)
                    dve.wait_ge(S["bu_done"], g + 1)
                    for k in range(KD):
                        dve.wait_ge(S["da_ready"], g * KD + k + 1)
                        for j in range(2):
                            one = slice(j * L, (j + 1) * L)
                            ins = dve.tensor_tensor_scan(bu[:, k, one], dA[:, k, one], bu[:, k, one], 0.0, ALU.mult,
                                                         ALU.add)
                        ins.then_inc(S["scan_done"], 1)
                    dve.wait_ge(S["scan_done"], g * KD + 1)
                    if first(name, b):
                        if c > 1:
                            dve.wait_ge(S["y_added"], c - 1)
                    elif c > 1:
                        dve.wait_ge(S["y_folded"], ((b - 1) * NC + c - 2) * KD + 1)
                    dve.wait_ge(S["c_copied"], g + 1)
                    dve.tensor_tensor(products(b, c)[:, 0, :], bu[:, 0, :], cs, ALU.mult).then_inc(S["prod_done"], 1)
                elif name == "x1":
                    if first(name, b):
                        dve.wait_ge(S["y_added"], NC)
                    else:
                        dve.wait_ge(S["y_folded"], b * NC * KD)
                    dve.wait_ge(ld_xT, b * 16 + 16)
                    ysum = acc if first(name, b) else y
                    for k in range(KD):
                        me.did(dve.scalar_tensor_tensor(y[:, k, :], u[:, k, :], dd[:, k:k + 1], ysum[:, k, :], ALU.mult,
                                                        ALU.add))
                    me.wait()
                    me.then(dve.tensor_tensor(y, y, sz[:], ALU.mult))
                    dve.tensor_tensor(x1[:, b % 2], y, x1[:, b % 2], ALU.add).then_inc(S["x1_done"], 1)
                elif name == "centre":
                    dve.wait_ge(S["mean_done"], b + 1)
                    me.then(dve.tensor_tensor(xc[:], x1[:, b % 2], misc[:, 0:1, :].broadcast_to([P, KD, L]), ALU.subtract))
                    dve.tensor_tensor(sq, xc[:], xc[:], ALU.mult).then_inc(S["sq_done"], 1)
                elif name == "norm":
                    dve.wait_ge(S["r2_done"], b + 1)
                    me.then(dve.scalar_tensor_tensor(n1, misc[:, 0, :], EPS, r2, ALU.add, ALU.mult))
                    me.then(dve.tensor_tensor(n2, n1, r2, ALU.mult))
                    me.then(dve.tensor_scalar(n1, n2, -0.5, 1.5, ALU.mult, ALU.add))
                    me.then(dve.tensor_tensor(n2, n1, r2, ALU.mult))
                    dve.tensor_tensor(xs[:], xc[:], n2.rearrange("p (o l) -> p o l", o=1).broadcast_to([P, KD, L]),
                                      ALU.mult).then_inc(S["xs_done"], 1)
                elif name == "xl":
                    dve.wait_ge(S["xh_done"], b + 1)
                    dve.tensor_tensor(xl[:, b % 2], xs[:], xh[:, b % 2].bitcast(F32), ALU.subtract).then_inc(S["xl_done"], 1)
                elif name == "top":
                    own.start(b)
                    dve.wait_ge(S["logits_done"], b + 1)
                    own.then(dve.tensor_tensor(lg[:, :, 0:NR], misc[:, :, 0:NR],
                                              rb.rearrange("p (o n) -> p o n", o=1).broadcast_to([P, 2, NR]), ALU.add))
                    dve.memset(sink[:], 0.0)
                    for t in range(2):
                        own.did(dve.max(m8[:, t, :], lg[:, t, 0:NR]))
                    own.wait()
                    dve.tensor_scalar(nm[:], m8[:, :, 0], -1.0, None, ALU.mult).then_inc(S["nm_done"], 1)
                elif name == "gates":
                    own.then(dve.memset(m8[:, :, TOPK:8], LOWEST))
                    dve.memset(sink[:], 0.0)
                    for t in range(2):
                        own.did(dve.match_replace(rep[:, t, :], m8[:, t, :], lg[:, t, :], HUGE))
                    own.wait()
                    own.then(dve.tensor_tensor(mask[:], rep[:, :, 0:NR], lg[:, :, 0:NR], ALU.not_equal))
                    dve.wait_ge(S["ex_done"], b + 1)
                    own.then(dve.tensor_tensor(em[:], ex[:], mask[:], ALU.mult))
                    own.then(dve.tensor_reduce(sm[:], em[:], AX.X, ALU.add))
                    own.then(dve.reciprocal(rsm[:], sm[:]))
                    for t in range(2):
                        own.did(dve.tensor_scalar(g34[:, t, 0:NR], em[:, t, :], rsm[:, t:t + 1], None, ALU.mult))
                    own.wait()
                    own.then(dve.tensor_copy(g3[:, :, 0, :], g34[:, :, 0:NR]))
                    own.then(dve.tensor_tensor(gr[:], g34[:, :, 0:NR], g3[:, :, 0, :], ALU.subtract))
                    own.then(dve.tensor_copy(g3[:, :, 1, :], gr[:]))
                    dve.tensor_tensor(g3[:, :, 2, :], gr[:], g3[:, :, 1, :], ALU.subtract).then_inc(S["g3_done"], 1)

            def pair(b, p, more):
                dve.wait_ge(S["relu_done"], b * NP + p + 1)
                n = len(PAIRS[p])
                if PAIRS[p][0] >= NT_S:
                    dve.wait_ge(S["gb_ready"], b * NPR + p - (NP - NPR) + 1)
                    ins = dve.tensor_tensor(hg[:, p % 4], hg[:, p % 4], gb[p % 2][:], ALU.mult)
                else:
                    ins = dve.tensor_scalar(hg[:, p % 4, 0:n], hg[:, p % 4, 0:n], 1.0 / NSH, None, ALU.mult)
                ins.then_inc(S["hg_done"], 1)
                if p and split(b, p - 1):
                    lower_h(b, p - 1)
                if more:
                    beside(p, step, b + 1)

            def lower_h(b, p):
                n = len(PAIRS[p])
                dve.wait_ge(S["hh_done"], nth_split(b, p))
                dve.tensor_tensor(hl[:, p % 4, 0:n], hg[:, p % 4, 0:n], hh[:, p % 4, 0:n].bitcast(F32),
                                  ALU.subtract).then_inc(S["hl_done"], 1)

            def end(b):
                if split(b, NP - 1):
                    lower_h(b, NP - 1)
                dve.wait_ge(S["acc_done"], b + 1)
                dve.tensor_tensor(x1[:, b % 2], acc[:], x1[:, b % 2], ALU.add).then_inc(S["ot_done"], 1)

            run(dve, pair, end, step)

        @block.gpsimd
        def _(pool):
            todo = list(range(NW))

            def split_w1(n):
                for i in todo[:n]:
                    a, e = i * WCH, min(NT, (i + 1) * WCH)
                    pool.wait_ge(w1h_done, i + 1)
                    pool.tensor_tensor(w1l[:, a:e, :].rearrange("p t m -> p (t m)"),
                                       stage[:, i % 2, 0:(e - a) * KD * P],
                                       w1h[:, a:e, :].rearrange("p t m -> p (t m)").bitcast(F32),
                                       ALU.subtract).then_inc(w1l_done, 1)
                del todo[:n]

            def step(name, b):
                if type(name) is tuple:
                    c = name[1]
                    g = b * NC + c
                    pool.wait_ge(S["c_copied"], g + 1)
                    pool.wait_ge(S["scan_done"], g * KD + 2)
                    if first(name, b):
                        if c > 1:
                            pool.wait_ge(S["y_added"], c - 1)
                    elif c > 1:
                        pool.wait_ge(S["y_folded"], ((b - 1) * NC + c - 2) * KD + 2)
                    pool.tensor_tensor(products(b, c)[:, 1, :], bu[:, 1, :], cs, ALU.mult).then_inc(S["pool_prod_done"], 1)
                    if first(name, b):
                        split_w1(1)
                    elif c:
                        for k in range(KD):
                            pool.wait_ge(S[("prod_done", "pool_prod_done")[k]], g + 1)
                            if c > 1:
                                pool.wait_ge(S["y_folded"], ((b - 1) * NC + c - 2) * KD + k + 1)
                            else:
                                pool.wait_ge(S[("prod_done", "pool_prod_done")[k]], g)
                            pool.tensor_tensor(ya[:, k, :], ya[:, k, :], pr[:, k, :], ALU.add).then_inc(S["y_folded"], 1)
                elif first(name, b):
                    if name in ("usig", "dtl", "sp"):
                        split_w1(1)
                    elif name == "x1":
                        split_w1(len(todo))
                elif name == "x1":
                    for k in range(KD):
                        pool.wait_ge(S["y_folded"], ((b - 1) * NC + NC - 2) * KD + k + 1)
                        pool.tensor_tensor(y[:, k, :], ya[:, k, 0:L], ya[:, k, L:2 * L],
                                           ALU.add).then_inc(S["y_folded"], 1)

            def pair(b, p, more):
                if more:
                    beside(p, step, b + 1)
                if split(b, p):
                    n = len(PAIRS[p])
                    pool.wait_ge(S["w2h_done"], nth_split(b, p))
                    pool.tensor_tensor(w2l[:, p % 4, 0:n, :], w2[:, p % RING, 0:n, :],
                                       w2h[:, p % 4, 0:n, :].bitcast(F32), ALU.subtract).then_inc(S["w2l_done"], 1)

            run(pool, pair, nothing, step)


def kernel(**inputs):
    import ml_dtypes
    import numpy as np
    import concourse.bacc as bacc
    from concourse.bass_utils import run_bass_kernel_spmd

    def get(n):
        return np.asarray(inputs[n])

    def halves(a):
        return a.reshape((KD, P) + a.shape[1:]).swapaxes(0, 1)

    x = get("x")
    xa = {k: get("L0_xattn_" + k) for k in ("in_proj_w", "conv_w", "conv_b", "x_proj_w", "dt_proj_w", "dt_proj_b",
                                            "A_log", "D")}
    ff = {k: get("L0_ffn_" + k) for k in ("sw1", "sb1", "sw2", "sb2", "rw1", "rb1", "rw2", "rb2", "router_w",
                                          "router_b")}
    f32 = x.dtype
    ns, off = NSH * HID, NT_S * P
    w1 = np.zeros((DX, NT * P), f32)
    w1[:, :ns] = ff["sw1"].transpose(1, 0, 2).reshape(DX, -1)
    w1[:, off:] = ff["rw1"].transpose(1, 0, 2).reshape(DX, -1)
    w2 = np.zeros((NT * P, DX), f32)
    w2[:ns] = ff["sw2"].reshape(-1, DX)
    w2[off:] = ff["rw2"].reshape(-1, DX)
    b1 = np.zeros((NT * P,), f32)
    b1[:ns] = ff["sb1"].reshape(-1)
    b1[off:] = ff["rb1"].reshape(-1)
    w1 = w1.reshape(KD, P, NT, P).transpose(1, 2, 0, 3).reshape(P, NT, KD * P)
    w2 = w2.reshape(NT, P, DX).transpose(1, 0, 2)
    xp = halves(xa["x_proj_w"].T)
    par = np.zeros((P, NPAR), f32)

    def put(name, a):
        par[:, PAR[name][0]:PAR[name][1]] = a.reshape(P, -1)

    put("win", xa["in_proj_w"].T)
    put("xbc", np.concatenate([xp[:, :, DR:]] * 3, axis=2))
    put("xdt", xp[:, :, :DR])
    put("cw", halves(xa["conv_w"]))
    put("cb", halves(xa["conv_b"]))
    put("dtb", halves(xa["dt_proj_b"]))
    put("alog", halves(xa["A_log"]))
    put("dd", halves(xa["D"]))
    put("rw", halves(ff["router_w"]))
    put("rb", np.broadcast_to(ff["router_b"], (P, NR)))
    put("b1", b1.reshape(NT, P).T)
    put("ident", np.eye(P, dtype=f32))
    small = np.zeros((NR + NSH, 2 * DX), f32)
    small[:DR, :DX] = xa["dt_proj_w"].T
    small[:NR, DX:] = ff["rb2"]
    small[NR:, DX:] = ff["sb2"]
    expert = np.arange(NR * HID) // HID
    selg = np.tile((expert[None, :] == np.arange(NR)[:, None]), (3, 1)).astype(ml_dtypes.bfloat16)
    selbc = np.tile(np.eye(2 * NS), (3, 1)).astype(ml_dtypes.bfloat16)
    arrays = {
        "in_xT": halves(x.transpose(2, 0, 1)),
        "in_xr": halves(x.transpose(1, 0, 2)).swapaxes(1, 2),
        "in_ctx": get("ctx_1024").transpose(2, 0, 1),
        "in_par": par,
        "in_small": small,
        "in_w1": w1,
        "in_w2": w2,
        "in_selg": selg.reshape(3 * NR, NT_R, P),
        "in_selbc": selbc,
    }
    arrays = {k: np.ascontiguousarray(a) for k, a in arrays.items()}
    nc = bacc.Bacc("TRN2", target_bir_lowering=False, num_devices=1, dynamic_dma_scratch_size=1024)
    args = [nc.dram_tensor(k, a.shape, mybir.dt.from_np(a.dtype), kind="ExternalInput").ap() for k, a in arrays.items()]
    out = nc.dram_tensor("out_0", (P, KD, B, L), F32, kind="ExternalOutput").ap()
    xattn_ffn_kernel(nc, *args, out)
    r = run_bass_kernel_spmd(nc, [arrays], core_ids=[0])
    o = r.results[0]["out_0"]
    return np.ascontiguousarray(o.transpose(2, 3, 1, 0).reshape(B, L, DX))
```
